# Optimizing a Trainium2 kernel written in Bass

```python
import numpy as np
import jax
import jax.numpy as jnp

def _softmax(x, axis=-1):
    return jax.nn.softmax(x, axis=axis)

def _gelu(x):
    return jax.nn.gelu(x, approximate=True)

def _silu(x):
    return jax.nn.silu(x)

def _sigmoid(x):
    return jax.nn.sigmoid(x)

def _layernorm(x, axis=-1, eps=1e-05):
    m = jnp.mean(x, axis=axis, keepdims=True)
    v = jnp.var(x, axis=axis, keepdims=True)
    return (x - m) / jnp.sqrt(v + eps)

def _scatter_add(tgt, idx, src, axis=0):
    return tgt.at[idx].add(src)

def _segment_sum(src, seg, n):
    return jax.ops.segment_sum(src, seg, n)
kernel_name = 'mk_perceiver_d1_seqx_r8_868649'

def setup_inputs(seed: int=0):
    np.random.seed(seed)
    _w = jnp.asarray

    def _rec_inputs():
        import jax
        import jax.numpy as jnp
        _rk = jax.random.key(seed)
        x = -0.0005146 + 1 * jax.random.normal(jax.random.fold_in(_rk, 1), (16, 32, 512), jnp.float32)
        _lenS = 32 - jax.random.randint(jax.random.fold_in(_rk, 7), (16,), 0, max(1, 32 // 4) + 1, jnp.int32)
        _lenS2 = 512 - jax.random.randint(jax.random.fold_in(_rk, 8), (16,), 0, max(1, 512 // 4) + 1, jnp.int32)
        _ctx_4096P = jax.random.normal(jax.random.fold_in(_rk, 11), (16, 16, 512), jnp.float32)
        _ctx_4096c = jax.random.dirichlet(jax.random.fold_in(_rk, 511), 0.3 * jnp.ones((16,), jnp.float32), (16, 512))
        _ctx_4096t = jnp.einsum('bsk,bkd->bsd', _ctx_4096c, _ctx_4096P)
        _ctx_4096t = _ctx_4096t * jax.lax.rsqrt(jnp.mean(jnp.square(_ctx_4096t)) + 1e-12) * 0.953939
        ctx_4096 = -0.0142356 + 1.00583 * (_ctx_4096t + 0.3 * jax.random.normal(jax.random.fold_in(_rk, 611), (16, 512, 512), jnp.float32))
        return (x, ctx_4096)
    x, ctx_4096 = _rec_inputs()

    def _L0_xattn_setup():
        import jax, jax.numpy as jnp
        import numpy as np
        K = 10
        NUM_BITS = 10
        M_METHODS = 4

        def _quantize(coords, num_bits=NUM_BITS):
            cmin = coords.min(axis=1, keepdims=True)
            cmax = coords.max(axis=1, keepdims=True)
            scale = (2 ** num_bits - 1) / (cmax - cmin + 1e-06)
            q = jnp.floor((coords - cmin) * scale)
            return jnp.clip(q, 0, 2 ** num_bits - 1).astype(jnp.int32)

        def _morton_key(q):
            x, y, z = (q[..., 0], q[..., 1], q[..., 2])
            key = jnp.zeros(x.shape, dtype=jnp.int32)
            for b in range(NUM_BITS):
                key = key | (x >> b & 1) << 3 * b + 2 | (y >> b & 1) << 3 * b + 1 | (z >> b & 1) << 3 * b
            return key

        def _hilbert_key(q, num_bits=NUM_BITS):
            n = 3
            X = [q[..., i] for i in range(n)]
            M = 1 << num_bits - 1
            Q = M
            while Q > 1:
                P = Q - 1
                for i in range(n):
                    cond = X[i] & Q > 0
                    t = (X[0] ^ X[i]) & P
                    new_X0 = jnp.where(cond, X[0] ^ P, X[0] ^ t)
                    if i != 0:
                        X[i] = jnp.where(cond, X[i], X[i] ^ t)
                    X[0] = new_X0
                Q >>= 1
            for i in range(1, n):
                X[i] = X[i] ^ X[i - 1]
            t = jnp.zeros_like(X[0])
            Q = M
            while Q > 1:
                t = jnp.where(X[n - 1] & Q > 0, t ^ Q - 1, t)
                Q >>= 1
            X = [xi ^ t for xi in X]
            key = jnp.zeros(X[0].shape, dtype=jnp.int32)
            for b in range(num_bits - 1, -1, -1):
                for i in range(n):
                    key = key << 1 | X[i] >> b & 1
            return key

        def _sorted_indices(coords_bn3):
            q = _quantize(coords_bn3)
            qt = q[..., jnp.array([1, 0, 2])]
            keys = [_morton_key(q), _morton_key(qt), _hilbert_key(q), _hilbert_key(qt)]
            return [jnp.argsort(kk, axis=1) for kk in keys]

        def _window_inds(sorted_idx, k=K):
            B, N = sorted_idx.shape
            i = jnp.arange(N)
            start = jnp.maximum(0, i - k // 2)
            end = jnp.minimum(N, i + k // 2 + 1)
            pos = jnp.minimum(start[:, None] + jnp.arange(k)[None, :], (end - 1)[:, None])
            return jnp.take(sorted_idx, pos, axis=1)

        def _get_graph_features(feats, inds_list, perm, W_lin, b_lin, k=K):
            B, N, C = feats.shape
            center = feats[:, :, None, :]
            gather = jax.vmap(lambda f, idx: f[idx])
            per_method = []
            for inds in inds_list:
                neigh = gather(feats, inds)
                gf = jnp.concatenate([jnp.broadcast_to(center, (B, N, k, C)), neigh - center], axis=-1)
                per_method.append(gf)
            allf = jnp.stack(per_method, axis=-1)
            allf = allf[..., perm]
            total = 2 * C * M_METHODS
            x = allf.reshape(B * N, k, total)
            x16 = x.astype(jnp.float16).astype(jnp.float32)
            headdim = min(32, total)
            nheads = total // headdim
            qh = x16.reshape(B * N, k, nheads, headdim)
            scores = jnp.einsum('bihd,bjhd->bhij', qh, qh) / np.float32(np.sqrt(headdim))
            attn = jax.nn.softmax(scores, axis=-1)
            out = jnp.einsum('bhij,bjhd->bihd', attn, qh).reshape(B * N, k, total)
            fused = out @ W_lin.T + b_lin
            return fused.reshape(B, N, k, 64)

        def _instance_norm(x, axes):
            mu = x.mean(axis=axes, keepdims=True)
            var = x.var(axis=axes, keepdims=True)
            return (x - mu) / jnp.sqrt(var + 1e-05)

        def _lrelu(x):
            return jnp.where(x > 0, x, 0.2 * x)
        key = jax.random.key(seed)
        ks = jax.random.split(key, 8)
        B, N, C = (2, 512, 32)
        tot = M_METHODS * 2 * C
        s = 0.02
        return {'coords': jax.random.normal(ks[0], (B, 3, N), jnp.float32), 'feats': jax.random.normal(ks[1], (B, C, N), jnp.float32), 'W_lin1': jax.random.normal(ks[2], (64, tot), jnp.float32) * s, 'b_lin1': jnp.zeros((64,), jnp.float32), 'W_lin2': jax.random.normal(ks[3], (64, tot), jnp.float32) * s, 'b_lin2': jnp.zeros((64,), jnp.float32), 'W_conv1': jax.random.normal(ks[4], (C, 2 * C), jnp.float32) * s, 'W_conv2': jax.random.normal(ks[5], (2 * C, 2 * C), jnp.float32) * s, 'W_conv3': jax.random.normal(ks[6], (C, 4 * C), jnp.float32) * s}
    _L0_xattn_all = _L0_xattn_setup()
    _L0_xattn_in = {k: v for k, v in _L0_xattn_all.items() if k in ('W_lin1', 'b_lin1', 'W_lin2', 'b_lin2', 'W_conv1', 'W_conv2', 'W_conv3')}
    del _L0_xattn_all

    def _L0_attn_setup():
        import jax, jax.numpy as jnp
        import numpy as np
        H = 32
        G = 8
        D = 128
        HID = 512
        THETA = 10000.0

        def _rope(x, pos):
            half = D // 2
            inv_freq = 1.0 / THETA ** (jnp.arange(0, half, dtype=jnp.float32) / half)
            ang = pos[:, None].astype(jnp.float32) * inv_freq[None, :]
            cos = jnp.cos(ang)[None, None]
            sin = jnp.sin(ang)[None, None]
            x1, x2 = (x[..., :half], x[..., half:])
            return jnp.concatenate([x1 * cos - x2 * sin, x1 * sin + x2 * cos], axis=-1)
        key = jax.random.key(seed)
        ks = jax.random.split(key, 9)
        s = 0.02
        return {'hidden_states': jax.random.normal(ks[0], (1, 256, HID), jnp.float32), 'Wq': jax.random.normal(ks[1], (HID, H * D), jnp.float32) * s, 'bq': jnp.zeros((H * D,), jnp.float32), 'Wk': jax.random.normal(ks[2], (HID, G * D), jnp.float32) * s, 'bk': jnp.zeros((G * D,), jnp.float32), 'Wv': jax.random.normal(ks[3], (HID, G * D), jnp.float32) * s, 'bv': jnp.zeros((G * D,), jnp.float32), 'Wo': jax.random.normal(ks[4], (H * D, HID), jnp.float32) * s, 'bo': jnp.zeros((HID,), jnp.float32)}
    _L0_attn_all = _L0_attn_setup()
    _L0_attn_in = {k: v for k, v in _L0_attn_all.items() if k in ('Wq', 'bq', 'Wk', 'bk', 'Wv', 'bv', 'Wo', 'bo')}
    del _L0_attn_all

    def _L0_ffn_setup():
        import jax, jax.numpy as jnp
        import numpy as np
        HID, BOT, RDIM, NSLOT, K, VB = (512, 64, 48, 128, 8, 32)
        TAU_LOW, TAU_HIGH, EARLY_EXIT = (0.5, 2.0, 0.05)

        def _uncertainty(h, Wu1, bu1, Wu2, bu2):
            var = jnp.var(h, axis=-1)
            log_var = jnp.log1p(var)
            norm_var = log_var / (jnp.mean(log_var) + 1e-06)
            learned = (jax.nn.gelu(h @ Wu1.T + bu1) @ Wu2.T + bu2)[..., 0]
            return jnp.clip(norm_var * 0.5 + jax.nn.sigmoid(learned) * 2.5, 0.0, 5.0)
        key = jax.random.key(seed)
        ks = jax.random.split(key, 12)
        B, S = (2, 256)
        return {'hidden_states': jax.random.normal(ks[0], (B, S, HID), dtype=jnp.float32), 'Wq': jax.random.normal(ks[1], (BOT, HID), dtype=jnp.float32) / np.sqrt(HID), 'Wr': jax.random.normal(ks[2], (RDIM, BOT), dtype=jnp.float32) / np.sqrt(BOT), 'aux_keys': jax.random.normal(ks[3], (NSLOT, BOT), dtype=jnp.float32) * 0.01, 'aux_values': jax.random.normal(ks[4], (NSLOT, HID), dtype=jnp.float32) * 0.02, 'Wvd': jax.random.normal(ks[5], (VB, HID), dtype=jnp.float32) * 0.1 / np.sqrt(HID), 'Wvu': jax.random.normal(ks[6], (HID, VB), dtype=jnp.float32) * 0.1 / np.sqrt(VB), 'Wu1': jax.random.normal(ks[7], (HID // 4, HID), dtype=jnp.float32) / np.sqrt(HID), 'bu1': jnp.zeros((HID // 4,), dtype=jnp.float32), 'Wu2': jax.random.normal(ks[8], (1, HID // 4), dtype=jnp.float32) * 0.01, 'bu2': jnp.zeros((1,), dtype=jnp.float32), 'gate_w1': jnp.float32(0.5), 'gate_bias': jnp.float32(-1.0), 'log_rel': jnp.zeros((NSLOT,), dtype=jnp.float32)}
    _L0_ffn_all = _L0_ffn_setup()
    _L0_ffn_in = {k: v for k, v in _L0_ffn_all.items() if k in ('Wq', 'Wr', 'aux_keys', 'aux_values', 'Wvd', 'Wvu', 'Wu1', 'bu1', 'Wu2', 'bu2', 'gate_w1', 'gate_bias', 'log_rel')}
    del _L0_ffn_all
    return {'x': x, 'ctx_4096': ctx_4096, 'L0_xattn_W_lin1': _L0_xattn_in['W_lin1'], 'L0_xattn_b_lin1': _L0_xattn_in['b_lin1'], 'L0_xattn_W_lin2': _L0_xattn_in['W_lin2'], 'L0_xattn_b_lin2': _L0_xattn_in['b_lin2'], 'L0_xattn_W_conv1': _L0_xattn_in['W_conv1'], 'L0_xattn_W_conv2': _L0_xattn_in['W_conv2'], 'L0_xattn_W_conv3': _L0_xattn_in['W_conv3'], 'L0_attn_Wq': _L0_attn_in['Wq'], 'L0_attn_bq': _L0_attn_in['bq'], 'L0_attn_Wk': _L0_attn_in['Wk'], 'L0_attn_bk': _L0_attn_in['bk'], 'L0_attn_Wv': _L0_attn_in['Wv'], 'L0_attn_bv': _L0_attn_in['bv'], 'L0_attn_Wo': _L0_attn_in['Wo'], 'L0_attn_bo': _L0_attn_in['bo'], 'L0_ffn_Wq': _L0_ffn_in['Wq'], 'L0_ffn_Wr': _L0_ffn_in['Wr'], 'L0_ffn_aux_keys': _L0_ffn_in['aux_keys'], 'L0_ffn_aux_values': _L0_ffn_in['aux_values'], 'L0_ffn_Wvd': _L0_ffn_in['Wvd'], 'L0_ffn_Wvu': _L0_ffn_in['Wvu'], 'L0_ffn_Wu1': _L0_ffn_in['Wu1'], 'L0_ffn_bu1': _L0_ffn_in['bu1'], 'L0_ffn_Wu2': _L0_ffn_in['Wu2'], 'L0_ffn_bu2': _L0_ffn_in['bu2'], 'L0_ffn_gate_w1': _L0_ffn_in['gate_w1'], 'L0_ffn_gate_bias': _L0_ffn_in['gate_bias'], 'L0_ffn_log_rel': _L0_ffn_in['log_rel']}

def reference(x, ctx_4096, L0_xattn_W_lin1, L0_xattn_b_lin1, L0_xattn_W_lin2, L0_xattn_b_lin2, L0_xattn_W_conv1, L0_xattn_W_conv2, L0_xattn_W_conv3, L0_attn_Wq, L0_attn_bq, L0_attn_Wk, L0_attn_bk, L0_attn_Wv, L0_attn_bv, L0_attn_Wo, L0_attn_bo, L0_ffn_Wq, L0_ffn_Wr, L0_ffn_aux_keys, L0_ffn_aux_values, L0_ffn_Wvd, L0_ffn_Wvu, L0_ffn_Wu1, L0_ffn_bu1, L0_ffn_Wu2, L0_ffn_bu2, L0_ffn_gate_w1, L0_ffn_gate_bias, L0_ffn_log_rel):
    import jax
    import jax.numpy as jnp

    def _L0_xattn_ref(coords, feats, W_lin1, b_lin1, W_lin2, b_lin2, W_conv1, W_conv2, W_conv3):
        import jax, jax.numpy as jnp
        import numpy as np
        K = 10
        NUM_BITS = 10
        M_METHODS = 4

        def _quantize(coords, num_bits=NUM_BITS):
            cmin = coords.min(axis=1, keepdims=True)
            cmax = coords.max(axis=1, keepdims=True)
            scale = (2 ** num_bits - 1) / (cmax - cmin + 1e-06)
            q = jnp.floor((coords - cmin) * scale)
            return jnp.clip(q, 0, 2 ** num_bits - 1).astype(jnp.int32)

        def _morton_key(q):
            x, y, z = (q[..., 0], q[..., 1], q[..., 2])
            key = jnp.zeros(x.shape, dtype=jnp.int32)
            for b in range(NUM_BITS):
                key = key | (x >> b & 1) << 3 * b + 2 | (y >> b & 1) << 3 * b + 1 | (z >> b & 1) << 3 * b
            return key

        def _hilbert_key(q, num_bits=NUM_BITS):
            n = 3
            X = [q[..., i] for i in range(n)]
            M = 1 << num_bits - 1
            Q = M
            while Q > 1:
                P = Q - 1
                for i in range(n):
                    cond = X[i] & Q > 0
                    t = (X[0] ^ X[i]) & P
                    new_X0 = jnp.where(cond, X[0] ^ P, X[0] ^ t)
                    if i != 0:
                        X[i] = jnp.where(cond, X[i], X[i] ^ t)
                    X[0] = new_X0
                Q >>= 1
            for i in range(1, n):
                X[i] = X[i] ^ X[i - 1]
            t = jnp.zeros_like(X[0])
            Q = M
            while Q > 1:
                t = jnp.where(X[n - 1] & Q > 0, t ^ Q - 1, t)
                Q >>= 1
            X = [xi ^ t for xi in X]
            key = jnp.zeros(X[0].shape, dtype=jnp.int32)
            for b in range(num_bits - 1, -1, -1):
                for i in range(n):
                    key = key << 1 | X[i] >> b & 1
            return key

        def _sorted_indices(coords_bn3):
            q = _quantize(coords_bn3)
            qt = q[..., jnp.array([1, 0, 2])]
            keys = [_morton_key(q), _morton_key(qt), _hilbert_key(q), _hilbert_key(qt)]
            return [jnp.argsort(kk, axis=1) for kk in keys]

        def _window_inds(sorted_idx, k=K):
            B, N = sorted_idx.shape
            i = jnp.arange(N)
            start = jnp.maximum(0, i - k // 2)
            end = jnp.minimum(N, i + k // 2 + 1)
            pos = jnp.minimum(start[:, None] + jnp.arange(k)[None, :], (end - 1)[:, None])
            return jnp.take(sorted_idx, pos, axis=1)

        def _get_graph_features(feats, inds_list, perm, W_lin, b_lin, k=K):
            B, N, C = feats.shape
            center = feats[:, :, None, :]
            gather = jax.vmap(lambda f, idx: f[idx])
            per_method = []
            for inds in inds_list:
                neigh = gather(feats, inds)
                gf = jnp.concatenate([jnp.broadcast_to(center, (B, N, k, C)), neigh - center], axis=-1)
                per_method.append(gf)
            allf = jnp.stack(per_method, axis=-1)
            allf = allf[..., perm]
            total = 2 * C * M_METHODS
            x = allf.reshape(B * N, k, total)
            x16 = x.astype(jnp.float16).astype(jnp.float32)
            headdim = min(32, total)
            nheads = total // headdim
            qh = x16.reshape(B * N, k, nheads, headdim)
            scores = jnp.einsum('bihd,bjhd->bhij', qh, qh) / np.float32(np.sqrt(headdim))
            attn = jax.nn.softmax(scores, axis=-1)
            out = jnp.einsum('bhij,bjhd->bihd', attn, qh).reshape(B * N, k, total)
            fused = out @ W_lin.T + b_lin
            return fused.reshape(B, N, k, 64)

        def _instance_norm(x, axes):
            mu = x.mean(axis=axes, keepdims=True)
            var = x.var(axis=axes, keepdims=True)
            return (x - mu) / jnp.sqrt(var + 1e-05)

        def _lrelu(x):
            return jnp.where(x > 0, x, 0.2 * x)
        inds_sorted = _sorted_indices(coords.transpose(0, 2, 1))
        inds_list = [_window_inds(s) for s in inds_sorted]
        perm1 = jnp.array([2, 0, 3, 1])
        perm2 = jnp.array([1, 3, 0, 2])
        f0 = feats.transpose(0, 2, 1)
        g1 = _get_graph_features(f0, inds_list, perm1, W_lin1, b_lin1)
        h1 = jnp.einsum('oc,bnkc->bonk', W_conv1, g1)
        h1 = _lrelu(_instance_norm(h1, (2, 3)))
        feats1 = h1.max(axis=-1)
        g2 = _get_graph_features(feats1.transpose(0, 2, 1), inds_list, perm2, W_lin2, b_lin2)
        h2 = jnp.einsum('oc,bnkc->bonk', W_conv2, g2)
        h2 = _lrelu(_instance_norm(h2, (2, 3)))
        feats2 = h2.max(axis=-1)
        f3 = jnp.concatenate([feats, feats1, feats2], axis=1)
        h3 = jnp.einsum('oc,bcn->bon', W_conv3, f3)
        return _lrelu(_instance_norm(h3, (2,)))

    def _L0_attn_ref(hidden_states, Wq, bq, Wk, bk, Wv, bv, Wo, bo):
        import jax, jax.numpy as jnp
        import numpy as np
        H = 32
        G = 8
        D = 128
        HID = 512
        THETA = 10000.0

        def _rope(x, pos):
            half = D // 2
            inv_freq = 1.0 / THETA ** (jnp.arange(0, half, dtype=jnp.float32) / half)
            ang = pos[:, None].astype(jnp.float32) * inv_freq[None, :]
            cos = jnp.cos(ang)[None, None]
            sin = jnp.sin(ang)[None, None]
            x1, x2 = (x[..., :half], x[..., half:])
            return jnp.concatenate([x1 * cos - x2 * sin, x1 * sin + x2 * cos], axis=-1)
        B, S, _ = hidden_states.shape
        R = H // G
        q = hidden_states @ Wq + bq
        k = hidden_states @ Wk + bk
        v = hidden_states @ Wv + bv
        q = q.reshape(B, S, H, D).transpose(0, 2, 1, 3)
        k = k.reshape(B, S, G, D).transpose(0, 2, 1, 3)
        v = v.reshape(B, S, G, D).transpose(0, 2, 1, 3)
        pos = jnp.arange(S)
        q = _rope(q, pos)
        k = _rope(k, pos)
        qg = q.reshape(B, G, R, S, D)
        scores = jnp.einsum('bgrsd,bgtd->bgrst', qg, k) / jnp.sqrt(jnp.float32(D))
        causal = jnp.tril(jnp.ones((S, S), dtype=bool))
        scores = jnp.where(causal[None, None, None], scores, jnp.finfo(scores.dtype).min)
        probs = jax.nn.softmax(scores, axis=-1)
        ctx = jnp.einsum('bgrst,bgtd->bgrsd', probs, v)
        ctx = ctx.reshape(B, H, S, D).transpose(0, 2, 1, 3).reshape(B, S, H * D)
        return ctx @ Wo + bo

    def _L0_ffn_ref(hidden_states, Wq, Wr, aux_keys, aux_values, Wvd, Wvu, Wu1, bu1, Wu2, bu2, gate_w1, gate_bias, log_rel):
        import jax, jax.numpy as jnp
        import numpy as np
        HID, BOT, RDIM, NSLOT, K, VB = (512, 64, 48, 128, 8, 32)
        TAU_LOW, TAU_HIGH, EARLY_EXIT = (0.5, 2.0, 0.05)

        def _uncertainty(h, Wu1, bu1, Wu2, bu2):
            var = jnp.var(h, axis=-1)
            log_var = jnp.log1p(var)
            norm_var = log_var / (jnp.mean(log_var) + 1e-06)
            learned = (jax.nn.gelu(h @ Wu1.T + bu1) @ Wu2.T + bu2)[..., 0]
            return jnp.clip(norm_var * 0.5 + jax.nn.sigmoid(learned) * 2.5, 0.0, 5.0)
        query = hidden_states @ Wq.T
        rq = query @ Wr.T
        rk = aux_keys @ Wr.T
        router_scores = jnp.einsum('bsr,nr->bsn', rq, rk) / np.sqrt(RDIM) + log_rel
        top_scores, top_idx = jax.lax.top_k(router_scores, K)
        sel_keys = aux_keys[top_idx]
        attn = jnp.einsum('bsd,bskd->bsk', query, sel_keys) / np.sqrt(BOT) + log_rel[top_idx]
        w = jax.nn.softmax(attn, axis=-1)
        sel_vals = aux_values[top_idx]
        aux_out = jnp.einsum('bsk,bskh->bsh', w, sel_vals)
        aux_out = aux_out @ Wvd.T @ Wvu.T
        u = _uncertainty(hidden_states, Wu1, bu1, Wu2, bu2)
        u_norm = jnp.clip((u - TAU_LOW) / (TAU_HIGH - TAU_LOW), 0.0, 1.0)
        gate = jax.nn.sigmoid(gate_w1 * u_norm + gate_bias)
        gate = jnp.where(gate < EARLY_EXIT, 0.0, gate)
        return hidden_states + gate[..., None] * aux_out
    x = x + _L0_xattn_ref(ctx_4096, _layernorm(x, axis=-1), L0_xattn_W_lin1, L0_xattn_b_lin1, L0_xattn_W_lin2, L0_xattn_b_lin2, L0_xattn_W_conv1, L0_xattn_W_conv2, L0_xattn_W_conv3)
    x = x + _L0_attn_ref(_layernorm(x, axis=-1), L0_attn_Wq, L0_attn_bq, L0_attn_Wk, L0_attn_bk, L0_attn_Wv, L0_attn_bv, L0_attn_Wo, L0_attn_bo)
    x = x + _L0_ffn_ref(_layernorm(x, axis=-1), L0_ffn_Wq, L0_ffn_Wr, L0_ffn_aux_keys, L0_ffn_aux_values, L0_ffn_Wvd, L0_ffn_Wvu, L0_ffn_Wu1, L0_ffn_bu1, L0_ffn_Wu2, L0_ffn_bu2, L0_ffn_gate_w1, L0_ffn_gate_bias, L0_ffn_log_rel)
    return x

_drawn_inputs = setup_inputs


def setup_inputs(seed=0):
    import zlib

    import numpy as np

    out = dict(_drawn_inputs(seed))
    spreads = {'L0_xattn_b_lin1': (0.0, 2.0),
     'L0_xattn_b_lin2': (0.0, 2.0),
     'L0_attn_bq': (0.0, 0.8),
     'L0_attn_bk': (0.0, 0.8),
     'L0_attn_bv': (0.0, 0.1),
     'L0_attn_bo': (0.0, 0.1),
     'L0_ffn_bu1': (0.0, 2.0),
     'L0_ffn_log_rel': (0.0, 2.0)}
    factors = {'L0_ffn_Wq': 62.602,
     'L0_ffn_Wr': 64.0,
     'L0_ffn_aux_keys': 60.759,
     'L0_ffn_aux_values': 60.758,
     'L0_ffn_Wvd': 60.104,
     'L0_ffn_Wvu': 59.341,
     'L0_ffn_Wu1': 64.0,
     'L0_ffn_Wu2': 64.0}
    for name, (base, spread) in spreads.items():
        noise = np.random.default_rng([zlib.crc32(name.encode()), seed]).standard_normal(out[name].shape)
        drawn = base * np.exp(spread * noise) if base else spread * noise
        out[name] = jnp.asarray(drawn.astype(out[name].dtype))
    for name, factor in factors.items():
        out[name] = (out[name] * factor).astype(out[name].dtype)
    return out
```

```python
import math
from contextlib import ExitStack

import numpy as np
import concourse.bass as bass
from concourse import mybir

F32 = mybir.dt.float32
F16 = mybir.dt.float16
BF16 = mybir.dt.bfloat16
I32 = mybir.dt.int32
ALU = mybir.AluOpType
ACT = mybir.ActivationFunctionType
AX = mybir.AxisListType.X

B, C, N = 16, 32, 512
M = 4
K = 10
BITS = 10
HD = 32
EPS = 1e-5
PERMS = ([2, 0, 3, 1], [1, 3, 0, 2])
OUTC = (32, 64)

PAIRS = B // 2
WIN = 16
TOK = 6
BLKS = 8
STEPT = BLKS * TOK
STEPS = -(-N // STEPT)
NCOL = STEPT * K
LASTT = N - (STEPS - 1) * STEPT
PADL = 5
POSW = 544
HG = 4
CH = N // 128
TW = STEPS * STEPT

NHEAD, NGRP, DH = 32, 8, 128
REP = NHEAD // NGRP
HID = 512
TOKENS = B * C
TILES = TOKENS // 128
KC = HID // 128

BOT, RDIM, NSLOT, VB = 64, 48, 128, 32


def constants():
    t = {}
    t["iota"] = np.broadcast_to(np.arange(N, dtype=np.float16), (128, N)).copy()
    p = np.arange(128)
    t["ident"] = np.eye(128, dtype=np.float32)
    t["headmask"] = ((p[:, None] % 32) // 8 == np.arange(4)[None, :]).astype(np.float32)
    t["tri"] = (np.arange(128)[None, :] < p[:, None]).astype(np.float32)
    t["group8"] = ((p // 64 * 4 + p % 4)[:, None] == np.arange(8)[None, :]).astype(np.float32)
    t["fold"] = (p[:, None] % 32 == np.arange(64)[None, :] % 32).astype(np.float32)
    w = p % 64 // HG
    blk, nl = np.arange(STEPT) // TOK, np.arange(STEPT) % TOK
    ok = (w[:, None] >= nl[None, :]) & (w[:, None] < nl[None, :] + K)
    std = np.where(ok, 0.0, 1e30).astype(np.float32)
    first = std.copy()
    for n in range(5):
        pos = w - PADL
        first[:, n] = np.where((pos >= 0) & (pos <= n + 5), 0.0, 1e30)
        first[pos == n + 5, n] = -math.log(5 - n) * math.sqrt(HD)
    t["keymask"] = np.stack([first, std], 1).reshape(128, 2 * STEPT).astype(np.float32)
    half = DH // 2
    inv = (1.0 / 10000.0 ** (np.arange(half, dtype=np.float32) / np.float32(half))).astype(np.float32)
    ang = np.arange(C, dtype=np.float32)[None, :] * inv[:, None]
    cos, sin = np.cos(ang).astype(np.float32), np.sin(ang).astype(np.float32)
    t["cos"] = np.concatenate([cos, cos], 0)
    t["sin"] = np.concatenate([sin, -sin], 0)
    s = p % 32
    t["causal"] = np.where(np.arange(32)[None, :] <= s[:, None], 0.0, -1e30).astype(np.float32)
    return t


def build(nc, io, out):
    ctx = ExitStack()

    def sb(name, shape, dt, c=ctx):
        return c.enter_context(nc.sbuf_tensor(name, shape, dt))

    def sem(name):
        return ctx.enter_context(nc.semaphore(name))

    def view(tensor, rows, offset, dims):
        a = tensor[rows, ...] if not isinstance(rows, slice) else tensor[rows]
        return bass.AP(tensor=a.tensor, offset=a.offset + offset, ap=[list(a.ap[0])] + [list(d) for d in dims])

    ps = [ctx.enter_context(nc.psum_tensor(f"bank{i}", [128, 512], F32)) for i in range(7)]
    ps_t = ctx.enter_context(nc.psum_tensor("bank_t", [128, 1024], F16))
    ps_ga, ps_v, ps_mt, ps_mb, ps_rb = ps[0:5]
    ps_o = ps[5:7]

    iota = sb("iota", [128, N], F16)
    ident = sb("ident", [128, 128], F32)
    ident_bf = sb("ident_bf", [128, 128], BF16)
    ident_h = sb("ident_h", [128, 128], F16)
    headmask = sb("headmask", [128, 4], F32)
    tri = sb("tri", [128, 128], F32)
    group8 = sb("group8", [128, 8], F32)
    fold = sb("fold", [128, 64], F32)
    keymask = sb("keymask", [128, 2 * STEPT], F32)
    eps_col = sb("eps_col", [128, 1], F32)
    started = sb("started", [128, 9], F32)
    small = {n: t for n, t in (("iota", iota), ("ident", ident), ("headmask", headmask), ("tri", tri),
                               ("group8", group8), ("fold", fold), ("keymask", keymask))}
    X = sb("X", [64, PAIRS, N], F32)

    g1 = ExitStack()
    F0 = sb("F0", [64, PAIRS, N], F32, g1)
    F1 = sb("F1", [64, PAIRS, N], F32, g1)
    rank = sb("rank", [128, B, M * CH], F32, g1)
    rank_p = sb("rank_p", [128, 2, M * CH], F32, g1)
    coord = sb("coord", [48, N], F32, g1)
    qf = sb("qf", [48, 3, N], F32, g1)
    qi = sb("qi", [48, N], I32, g1)
    cs = sb("cs", [48, 8], F32, g1)
    XQ = sb("XQ", [128, 3, 64], I32, g1)
    HX = sb("HX", [128, 3, 2, 64], I32, g1)
    hm = sb("hm", [128, 4, 2, 64], I32, g1)
    SP1 = sb("SP1", [128, 3, 3, 64], I32, g1)
    KEY = sb("KEY", [128, M, 64], I32, g1)
    KEYT = sb("KEYT", [128, M, 64], I32, g1)
    K64 = sb("K64", [64, N], F32, g1)
    kcol = sb("kcol", [128, CH, 64], F32, g1)
    kb_ring = sb("kb_ring", [128, 2, M, N], F32, g1)
    cmp = sb("cmp", [128, 4, N], F16, g1)
    cnt = sb("cnt", [128, 3, M * CH], F32, g1)
    st = sb("st", [128, STEPS, 6], F32, g1)
    stx = sb("stx", [64, PAIRS, 6], F32, g1)
    mv = sb("mv", [128, PAIRS, 2], F32, g1)
    rs = sb("rs", [128, PAIRS, 2], F32, g1)
    P1H = sb("P1H", [128, 2, M, CH, N], F16, g1)
    FS = sb("FS", [64, 2, N], F16, g1)
    C2 = sb("C2", [65, TW], F32, g1)
    TT = sb("TT", [128, CH, 2, 64], F16, g1)
    R = sb("R", [128, 2, 2, 2, POSW], F16, g1)
    LB = sb("LB", [128, 2, 2, POSW, HG], F16, g1)
    FW = sb("FW", [128, 2, BLKS, 128], F32, g1)
    aM = sb("aM", [128, STEPT], F32, g1)
    S = sb("S", [128, 2, NCOL], F32, g1)
    A = sb("A", [128, 2, NCOL], F32, g1)
    AN = sb("AN", [128, 2, NCOL], F32, g1)
    MTs = sb("MTs", [120, 4 * 8], BF16, g1)
    MTe = sb("MTe", [120, 4 * 128], BF16, g1)
    rZe = sb("rZe", [120, 4 * 128], F32, g1)
    rZ = sb("rZ", [120, 4 * 8], F32, g1)
    Vbd = sb("Vbd", [128, 2, BLKS * 128], F32, g1)
    raw = sb("raw", [128, TW], F32, g1)
    fy = sb("fy", [128, N], F32, g1)
    F2 = sb("F2", [128, N], F32, g1)
    h3 = sb("h3", [64, N], F32, g1)
    Wl = [sb(f"Wl{i}", [64, 256], F32, g1) for i in range(2)]
    Wc = [sb(f"Wc{i}", [64, OUTC[i]], F32, g1) for i in range(2)]
    bl = [sb(f"bl{i}", [64, 1], F32, g1) for i in range(2)]
    WD = [sb(f"WD{i}", [128, OUTC[i]], F32, g1) for i in range(2)]
    W4 = [sb(f"W4{i}", [128, OUTC[i]], F32, g1) for i in range(2)]
    Wcc = [sb(f"Wcc{i}", [65, 2 * OUTC[i]], F32, g1) for i in range(2)]
    W3a = sb("W3a", [64, 64], F32, g1)
    W3b = sb("W3b", [64, 64], F32, g1)
    W3c = sb("W3c", [128, 64], F32, g1)
    XS = sb("XS", [128, 3, 3, 64], I32, g1)
    kc_b = sb("kc_b", [128, M, CH], F32, g1)
    g1.close()

    g2 = ExitStack()
    XN = sb("XN", [128, TILES, HID], F32, g2)
    LN = sb("LN", [128, TILES, HID], F32, g2)
    XT = sb("XT", [128, KC, TOKENS], F32, g2)
    wqkv = sb("wqkv", [128, 2, KC, (REP + 2) * DH], F32, g2)
    wo = sb("wo", [128, 2, REP, HID], F32, g2)
    bq = sb("bq", [128, NHEAD], F32, g2)
    bk = sb("bk", [128, NGRP], F32, g2)
    bv = sb("bv", [1, NGRP * DH], F32, g2)
    bo = sb("bo", [1, HID], F32, g2)
    ones_row = sb("ones_row", [1, 128], F32, g2)
    cosT = sb("cosT", [128, C], F32, g2)
    sinT = sb("sinT", [128, C], F32, g2)
    causal = sb("causal", [128, C], F32, g2)
    r1 = sb("r1", [128, 2, TOKENS], F32, g2)
    r2 = sb("r2", [128, 2, TOKENS], F32, g2)
    kT = sb("kT", [128, TOKENS], F32, g2)
    qT = sb("qT", [128, B, REP, C], F32, g2)
    vt = sb("vt", [128, TILES, DH], F32, g2)
    pr = sb("pr", [128, B, C], F32, g2)
    pm = sb("pm", [128, 3, B], F32, g2)
    PT = sb("PT", [128, TILES, 4, 128], F32, g2)
    CT = sb("CT", [128, TILES, REP, 4, C], F32, g2)
    st2 = sb("st2", [128, TILES, 6], F32, g2)
    mv2 = sb("mv2", [128, TILES, 2], F32, g2)
    rs2 = sb("rs2", [128, TILES, 2], F32, g2)
    fWq = sb("fWq", [128, KC, BOT], F32, g2)
    fWr = sb("fWr", [BOT, RDIM], F32, g2)
    akT = sb("akT", [BOT, NSLOT], F32, g2)
    avT = sb("avT", [128, KC, NSLOT], F32, g2)
    wvd = sb("wvd", [128, KC, VB], F32, g2)
    wvu = sb("wvu", [VB, HID], F32, g2)
    wu1 = sb("wu1", [128, KC, 128], F32, g2)
    bu1 = sb("bu1", [128, 1], F32, g2)
    wu2 = sb("wu2", [128, 1], F32, g2)
    lrel = sb("lrel", [128, NSLOT], F32, g2)
    sc3 = sb("sc3", [128, 3], F32, g2)
    ones_sq = sb("ones_sq", [128, 128], F32, g2)
    quT = sb("quT", [BOT, TOKENS], F32, g2)
    rqT = sb("rqT", [RDIM, TOKENS], F32, g2)
    rkT = sb("rkT", [RDIM, NSLOT], F32, g2)
    t1T = sb("t1T", [VB, NSLOT], F32, g2)
    AV = sb("AV", [NSLOT, HID], F32, g2)
    gl = sb("gl", [128, 4, TOKENS], F32, g2)
    rt = sb("rt", [128, TILES, NSLOT], F32, g2)
    rp = sb("rp", [128, TILES, NSLOT], F32, g2)
    at = sb("at", [128, TILES, NSLOT], F32, g2)
    wT = sb("wT", [128, TILES, 128], F32, g2)
    top = sb("top", [128, TILES, 8], F32, g2)
    gt = sb("gt", [128, 12, TILES], F32, g2)
    bg = sb("bg", [128, REP + 1], F32, g2)
    g2.close()

    consts_in = sem("consts_in")
    x_in = sem("x_in")
    coord_in = sem("coord_in")
    w_in = sem("w_in")
    vec = sem("vec_order")
    act_order = sem("act_order")
    pool_order = sem("pool_order")
    casts_done = sem("casts_done")
    zeros_done = sem("zeros_done")
    q_ready = sem("q_ready")
    q_out = sem("q_out")
    q_back = sem("q_back")
    key_ready = sem("key_ready")
    key_out = sem("key_out")
    key_back = sem("key_back")
    key_turned = sem("key_turned")
    kcol_ready = sem("kcol_ready")
    kb_in = [sem(f"kb_in{i}") for i in range(2)]
    kb_used = sem("kb_used")
    weff_mm = sem("weff_mm")
    weff_ev = sem("weff_ev")
    ln_var = sem("ln_var")
    ln_std = sem("ln_std")
    pair_done = sem("pair_done")
    fs_ready = sem("fs_ready")
    ctr_in = sem("ctr_in")
    turned = sem("turned")
    tt_ready = sem("tt_ready")
    onehot_ready = sem("onehot_ready")
    perm_mm = sem("perm_mm")
    perm_ev = sem("perm_ev")
    lb_ready = sem("lb_ready")
    fw_ready = sem("fw_ready")
    mte_ready = sem("mte_ready")
    rze_ready = sem("rze_ready")
    pad_ready = sem("pad_ready")
    ga_ready = sem("ga_ready")
    v_ready = sem("v_ready")
    vbd_ready = sem("vbd_ready")
    s_ready = sem("s_ready")
    mt_ready = sem("mt_ready")
    mts_ready = sem("mts_ready")
    mb_ready = sem("mb_ready")
    d_ready = sem("d_ready")
    e_ready = sem("e_ready")
    z_ready = sem("z_ready")
    rz_ready = sem("rz_ready")
    rb_ready = sem("rb_ready")
    an_ready = sem("an_ready")
    o_ready = sem("o_ready")
    o_used = sem("o_used")
    var_ready = sem("var_ready")
    std_ready = sem("std_ready")
    f2_ready = sem("f2_ready")
    h3_mm = sem("h3_mm")
    layer_zero = sem("layer_zero")
    graph_done = sem("graph_done")
    xn_in = sem("xn_in")
    aw_in = sem("aw_in")
    fw_in = sem("fw_in")
    wqkv_in = [sem(f"wqkv_in{i}") for i in range(2)]
    wo_in = [sem(f"wo_in{i}") for i in range(2)]
    wo_used = sem("wo_used")
    fill2 = sem("fill2")
    ln2_var = sem("ln2_var")
    ln2_std = sem("ln2_std")
    ln2_ready = sem("ln2_ready")
    xt_mm = sem("xt_mm")
    xt_ready = sem("xt_ready")
    proj_mm = sem("proj_mm")
    rope_parts = sem("rope_parts")
    qk_ready = sem("qk_ready")
    v_mm = sem("v_mm")
    vt_ready = sem("vt_ready")
    sc_mm = sem("sc_mm")
    sm_ready = sem("sm_ready")
    ex_ready = sem("ex_ready")
    pr_ready = sem("pr_ready")
    pt_mm = sem("pt_mm")
    pt_ready = sem("pt_ready")
    ctx_mm = sem("ctx_mm")
    ct_ready = sem("ct_ready")
    acc_mm = sem("acc_mm")
    ffn_mm = sem("ffn_mm")
    ffn_act = sem("ffn_act")
    ffn_vec = sem("ffn_vec")
    out_written = sem("out_written")
    kc_ready = sem("kc_ready")
    compared = sem("compared")
    COMPARES = M * (3 * CH - 1)
    rank_ready = sem("rank_ready")
    w4_ready = sem("w4_ready")
    am_ready = sem("am_ready")
    prep = sem("prep")
    fin = sem("fin")
    tail = sem("tail")
    soft = sem("soft")
    bg_ready = sem("bg_ready")
    row_ready = sem("row_ready")
    PREP, TAIL, SOFT = 3, 5, 4

    q_dram = nc.dram_tensor("q_scratch", [3, B * N], I32, kind="Internal").ap()
    k_dram = nc.dram_tensor("key_scratch", [M, B * N], I32, kind="Internal").ap()

    class Order:

        def __init__(self, eng, s):
            self.eng, self.s, self.n = eng, s, 0

        def did(self, ins):
            ins.then_inc(self.s, 1)
            self.n += 1
            return ins

        def sync(self):
            self.eng.wait_ge(self.s, self.n)

        def step(self, ins):
            self.did(ins)
            self.sync()

    block = ctx.enter_context(nc.Block())
    from_pairs = lambda a: a.rearrange("(q b) c n -> (b c) q n", b=2)

    @block.sync
    def _(sp):
        for d in range(3):
            sp.dma_start(coord[B * d:B * d + B, :], io["ctx_4096"][:, d, :]).then_inc(coord_in, 16)
        for name, tile in small.items():
            sp.dma_start(tile[:, :], io[name]).then_inc(consts_in, 16)
        sp.dma_start(X[:, :, :], from_pairs(io["x"])).then_inc(x_in, 16)
        for i in range(2):
            sp.dma_start(Wl[i][:, :], io[f"wlin{i}"]).then_inc(w_in, 16)
            sp.dma_start(Wc[i][:, :], io[f"wconv{i}T"]).then_inc(w_in, 16)
            sp.dma_start(bl[i][:, :], io[f"blin{i}"].rearrange("(k a) -> k a", a=1)).then_inc(w_in, 16)
        sp.wait_ge(zeros_done, 1)
        for b in range(2):
            r, c = slice(32 * b, 32 * b + 32), slice(32 * b, 32 * b + 32)
            sp.dma_start(W3a[r, c], io["wconv3T"][0:32, :]).then_inc(w_in, 16)
            sp.dma_start(W3b[r, c], io["wconv3T"][32:64, :]).then_inc(w_in, 16)
            sp.dma_start(W3c[64 * b:64 * b + 64, c], io["wconv3T"][64:128, :]).then_inc(w_in, 16)
        sp.wait_ge(q_ready, 1)
        for d in range(3):
            sp.dma_start(q_dram[d, :].rearrange("(b n) -> b n", n=N), qi[B * d:B * d + B, :]).then_inc(q_out, 16)
        sp.wait_ge(q_out, 48)
        sp.dma_start(XQ[:, :, :], q_dram.rearrange("d (p n) -> p d n", n=64)).then_inc(q_back, 16)
        sp.wait_ge(key_ready, 1)
        sp.dma_start(k_dram.rearrange("m (p n) -> p m n", n=64), KEY[:, :, :]).then_inc(key_out, 16)
        sp.wait_ge(key_out, 16)
        for m in range(M):
            sp.dma_start(K64[B * m:B * m + B, :], k_dram[m, :].rearrange("(b n) -> b n", n=N).bitcast(F32))\
              .then_inc(key_back, 16)
        with sp.Fori(0, B // 2) as h:
            for u in range(2):
                sp.wait_ge(kb_used, 1 + h * 2)
                sp.dma_start(kb_ring[:, u, :, :],
                             k_dram[:, bass.ds(h * 2 * N + u * N, N)].bitcast(F32).partition_broadcast(128))\
                  .then_inc(kb_in[u], 16)
        for L in range(2):
            with sp.Fori(0, PAIRS) as q:
                sp.wait_ge(fs_ready, q + (L * PAIRS + 1))
                for b in range(2):
                    for m in range(M):
                        sp.dma_start(R[32 * m:32 * m + 32, b, :, 1, 0:N], FS[32 * b:32 * b + 32, :, :])\
                          .then_inc(ctr_in, 16)
        sp.wait_ge(graph_done, 1)
        for u in range(2):
            sp.dma_start(XN[64 * u:64 * u + 64, :, :], X[:, :, :].rearrange("p (t u) n -> p u t n", u=2)[:, u, :, :])\
              .then_inc(xn_in, 16)
        for tile, name in ((cosT, "cos"), (sinT, "sin"), (causal, "causal")):
            sp.dma_start(tile[:, :], io[name]).then_inc(aw_in, 16)
        sp.dma_start(bq[:, :], io["bqT"]).then_inc(aw_in, 16)
        sp.dma_start(bk[:, :], io["bkT"]).then_inc(aw_in, 16)
        sp.dma_start(bv[:, :], io["bv"].rearrange("(a n) -> a n", a=1)).then_inc(aw_in, 16)
        sp.dma_start(bo[:, :], io["bo"].rearrange("(a n) -> a n", a=1)).then_inc(aw_in, 16)
        wq_v = io["Wq"].rearrange("(k p) n -> p k n", p=128)
        wk_v = io["Wk"].rearrange("(k p) n -> p k n", p=128)
        wv_v = io["Wv"].rearrange("(k p) n -> p k n", p=128)
        wo_v = io["Wo"].rearrange("(h p) n -> p h n", p=128)
        with sp.Fori(0, NGRP // 2) as h:
            for u in range(2):
                sp.wait_ge(v_mm, 1 + h * 2)
                sp.dma_start(wqkv[:, u, :, 0:REP * DH],
                             wq_v[:, :, bass.ds(h * (2 * REP * DH) + u * REP * DH, REP * DH)]).then_inc(wqkv_in[u], 16)
                sp.dma_start(wqkv[:, u, :, REP * DH:(REP + 1) * DH],
                             wk_v[:, :, bass.ds(h * (2 * DH) + u * DH, DH)]).then_inc(wqkv_in[u], 16)
                sp.dma_start(wqkv[:, u, :, (REP + 1) * DH:],
                             wv_v[:, :, bass.ds(h * (2 * DH) + u * DH, DH)]).then_inc(wqkv_in[u], 16)
                sp.wait_ge(wo_used, 1 + h * 2)
                sp.dma_start(wo[:, u, :, :], wo_v[:, bass.ds(h * (2 * REP) + u * REP, REP), :]).then_inc(wo_in[u], 16)
        kp = lambda a: a.rearrange("(k p) n -> p k n", p=128)
        for tile, src in ((fWq, kp(io["fWqT"])), (avT, kp(io["avT"])), (wvd, kp(io["WvdT"])), (wu1, kp(io["Wu1T"])),
                          (fWr, io["WrT"]), (akT, io["akT"]), (wvu, io["WvuT"]),
                          (bu1, io["bu1"].rearrange("(p a) -> p a", a=1)), (wu2, io["Wu2T"]),
                          (lrel, io["log_rel"].partition_broadcast(128))):
            sp.dma_start(tile[...], src).then_inc(fw_in, 16)
        for i, name in enumerate(("bu2", "gate_w1", "gate_bias")):
            sp.dma_start(sc3[:, i:i + 1], io[name].partition_broadcast(128)).then_inc(fw_in, 16)
        tokens = lambda a: a.rearrange("(t b) c n -> (b c) t n", b=4)
        for t in range(TILES):
            sp.wait_ge(row_ready, t + 1)
            sp.dma_start(tokens(out)[:, t, :], XN[:, t, :]).then_inc(out_written, 16)
        sp.wait_ge(out_written, 16 * TILES)

    @block.gpsimd
    def _(pool):
        o = Order(pool, pool_order)
        for t in (W3a, W3b, W3c, Wcc[0], Wcc[1], Vbd):
            o.did(pool.memset(t[...], 0.0))
        o.did(pool.memset(R[:, :, :, 1, :], 0.0))
        o.did(pool.memset(C2[0:64, N:TW], 0.0))
        o.sync()
        o.step(pool.memset(C2[64:65, :], 1.0))
        o.did(pool.memset(eps_col[:, :], EPS))
        for i, s in enumerate((pair_done, kb_used, v_mm, wo_used, sc_mm, ctx_mm, qk_ready, ct_ready, pt_ready)):
            pool.memset(started[:, i:i + 1], 0.0).then_inc(s, 1)
        o.sync()
        pool.wait_ge(consts_in, 16 * len(small))
        o.did(pool.tensor_copy(ident_bf[:, :], ident[:, :]))
        o.did(pool.tensor_copy(ident_h[:, :], ident[:, :]))
        o.sync()
        pool.memset(cnt[:, :, :], 0.0).then_inc(zeros_done, 1)
        for L in range(2):
            if L == 1:
                pool.wait_ge(pair_done, 1 + PAIRS)
                pool.memset(Vbd[:, :, :], 0.0).then_inc(layer_zero, 1)
            with pool.Fori(0, PAIRS) as q:
                idx = q + L * PAIRS
                base = q * STEPS + L * PAIRS * STEPS
                for b in range(2):
                    pool.wait_ge(pad_ready, idx * 2 + (b + 1))
                    pool.nop(nofuse=True)
                    for h in range(HG):
                        ins = pool.tensor_scalar(LB[:, b, :, :, h], R[:, b, :, 0, :], headmask[:, h:h + 1], 1.0,
                                                 ALU.mult, ALU.mult)
                ins.then_inc(lb_ready, 1)
                pool.wait_ge(lb_ready, idx + 1)
                for t in range(STEPS):
                    if t >= 2:
                        pool.wait_ge(v_ready, base + (t - 1))
                    for b in range(2):
                        win = [view(LB, slice(0, 128), ((b * 2 + part) * POSW + t * STEPT) * HG,
                                    [[TOK * HG, BLKS], [1, 64]]) for part in range(2)]
                        ins = pool.tensor_tensor(FW[:, t % 2, :, 64 * b:64 * b + 64], win[0], win[1], ALU.add)
                    ins.then_inc(fw_ready, 1)
        pool.wait_ge(graph_done, 1)
        pool.memset(PT[...], 0.0).then_inc(fill2, 1)
        pool.memset(ones_row[:, :], 1.0).then_inc(fill2, 1)
        pool.memset(ones_sq[:, :], 1.0).then_inc(fill2, 1)
        with pool.Fori(0, NGRP) as g:
            for j in range(REP + 1):
                pool.wait_ge(rope_parts, g * (REP + 1) + j + 1)
                if j == 0:
                    pool.wait_ge(sc_mm, 1 + g)
                dst = kT[:, :] if j == 0 else qT[:, :, j - 1, :]
                by_b = (lambda a: a) if j == 0 else (lambda a: a.rearrange("p (b s) -> p b s", b=B))
                pool.tensor_tensor(dst, by_b(r1[:, j % 2, :]), by_b(r2[:, j % 2, :]), ALU.add).then_inc(qk_ready, 1)

    @block.scalar
    def _(act):
        for L in range(2):
            oc = OUTC[L]
            act.wait_ge(weff_mm, 3 * L + 1)
            act.activation(WD[L][:, :], ps_ga[:, 0:oc], ACT.Copy).then_inc(weff_ev, 1)
            act.wait_ge(weff_mm, 3 * L + 2)
            act.wait_ge(zeros_done, 1)
            act.activation(Wcc[L][0:32, 0:oc], ps_v[0:32, 0:oc], ACT.Copy).then_inc(act_order, 1)
            act.activation(Wcc[L][32:64, oc:2 * oc], ps_v[32:64, 0:oc], ACT.Copy).then_inc(act_order, 1)
            act.wait_ge(weff_mm, 3 * L + 3)
            act.activation(Wcc[L][64:65, 0:oc], ps_v[64:65, 0:oc], ACT.Copy).then_inc(act_order, 1)
            act.activation(Wcc[L][64:65, oc:2 * oc], ps_v[64:65, 0:oc], ACT.Copy).then_inc(weff_ev, 1)
        act.wait_ge(key_turned, 1)
        act.activation(kcol[:, :, :], ps_mt[:, 0:CH * 64].rearrange("p (c k) -> p c k", c=CH), ACT.Copy)\
           .then_inc(kcol_ready, 1)
        act.wait_ge(ln_var, 1)
        act.activation(rs[0:64, :, 0], mv[0:64, :, 1], ACT.Sqrt, bias=eps_col[0:64, :]).then_inc(ln_std, 1)

        def over_window(tile, group, key, head):
            return view(tile, slice(0, 120), 0, [[group, 8], [key, WIN], [head, HG]])

        def v_blocks(L, base, t):
            oc = OUTC[L]
            act.wait_ge(v_ready, base + (t + 1))
            if t >= 2:
                act.wait_ge(o_ready, base + (t - 1))
            for b in range(2):
                r = slice(64 * b, 64 * b + 64)
                dst = Vbd[r, t % 2, 0:BLKS * 2 * oc].rearrange("p (k o) -> p k o", k=BLKS)[:, :, b * oc:b * oc + oc]
                ins = act.activation(dst, ps_v[r, 0:BLKS * oc].rearrange("p (k o) -> p k o", k=BLKS), ACT.Copy)
            ins.then_inc(vbd_ready, 1)

        for L in range(2):
            if L == 1:
                act.wait_ge(layer_zero, 1)
            with act.Fori(0, PAIRS) as q:
                idx = q + L * PAIRS
                base = q * STEPS + L * PAIRS * STEPS
                act.wait_ge(pair_done, 1 + idx)
                act.wait_ge(turned, idx + 1)
                act.activation(TT[:, :, :, :], ps_t[:, 0:CH * 128].rearrange("p (c h k) -> p c h k", c=CH, h=2),
                               ACT.Copy).then_inc(tt_ready, 1)
                for b in range(2):
                    act.wait_ge(perm_mm, idx * 2 + (b + 1))
                    hi, lo = ((ps_mt, ps_mb), (ps_rb, ps_o[0]))[b]
                    act.activation(R[:, b, 0, 0, PADL:PADL + N], hi[:, :], ACT.Copy).then_inc(perm_ev, 1)
                    act.activation(R[:, b, 1, 0, PADL:PADL + N], lo[:, :], ACT.Copy).then_inc(perm_ev, 1)
                v_blocks(L, base, 0)
                for t in range(STEPS + 1):
                    if t >= 1:
                        act.wait_ge(rz_ready, base + t)
                        if t >= 2:
                            act.wait_ge(rb_ready, base + (t - 1))
                        act.activation(over_window(rZe, HG * WIN, HG, 1), over_window(rZ, HG, 0, 1), ACT.Copy)\
                           .then_inc(rze_ready, 1)
                    if t == STEPS:
                        break
                    act.wait_ge(mts_ready, base + (t + 1))
                    if t >= 1:
                        act.wait_ge(mb_ready, base + t)
                    act.activation(over_window(MTe, HG * WIN, HG, 1), over_window(MTs, HG, 0, 1), ACT.Copy)\
                       .then_inc(mte_ready, 1)
                    if t + 1 < STEPS:
                        v_blocks(L, base, t + 1)
                    act.wait_ge(d_ready, base + (t + 1))
                    if t >= 2:
                        act.wait_ge(an_ready, base + (t - 1))
                    act.activation(A[:, t % 2, :], S[:, t % 2, :], ACT.Exp, scale=1.0 / math.sqrt(HD))\
                       .then_inc(e_ready, 1)
                act.wait_ge(var_ready, idx + 1)
                rows = 2 * OUTC[L]
                act.activation(rs[0:rows, 0, 0:1], mv[0:rows, 0, 1:2], ACT.Sqrt, bias=eps_col[0:rows, :])\
                   .then_inc(std_ready, 1)
                if L == 1:
                    act.wait_ge(h3_mm, q + 1)
                    act.wait_ge(f2_ready, 2 * q + 2)
                    act.activation(rs[0:64, 1, 0:1], mv[0:64, 1, 1:2], ACT.Sqrt, bias=eps_col[0:64, :])\
                       .then_inc(ln_std, 1)
        act.wait_ge(ln2_var, 1)
        act.activation(rs2[:, :, 0], mv2[:, :, 1], ACT.Sqrt, bias=eps_col[:, :]).then_inc(ln2_std, 1)
        for k in range(KC):
            act.wait_ge(xt_mm, k + 1)
            act.activation(XT[:, k, :], ps[k][:, :], ACT.Copy).then_inc(xt_ready, 1)
        with act.Fori(0, NGRP) as g:
            act.wait_ge(v_mm, 1 + g + 1)
            act.wait_ge(ctx_mm, 1 + g * TILES)
            act.activation(vt[:, :, :], ps[6][:, :].rearrange("p (t d) -> p t d", t=TILES), ACT.Copy)\
               .then_inc(vt_ready, 1)
            act.wait_ge(sm_ready, g + 1)
            act.activation(pr[:, :, :], pr[:, :, :], ACT.Exp).then_inc(ex_ready, 1)
            act.wait_ge(pt_mm, g + 1)
            for b in range(4):
                r = slice(32 * b, 32 * b + 32)
                ins = act.activation(PT[r, :, b, :], ps[6][r, :].rearrange("p (t k) -> p t k", t=TILES), ACT.Copy)
            ins.then_inc(pt_ready, 1)
            for t in range(TILES):
                act.wait_ge(ctx_mm, 1 + g * TILES + (t + 1))
                if t == 0:
                    act.wait_ge(wo_used, 1 + g)
                act.activation(CT[:, t, :, :, :].rearrange("p r b s -> p b r s"), ps[4 + t % 2][:, :].rearrange("p (b r s) -> p b r s", b=4, r=REP),
                               ACT.Copy).then_inc(ct_ready, 1)
        act.wait_ge(ln2_var, 2)
        act.activation(rs2[:, :, 0], mv2[:, :, 1], ACT.Sqrt, bias=eps_col[:, :]).then_inc(ln2_std, 1)
        for k in range(KC):
            act.wait_ge(xt_mm, KC + k + 1)
            act.activation(XT[:, k, :], ps[k][:, :], ACT.Copy).then_inc(xt_ready, 1)
        act.wait_ge(ffn_mm, 1)
        act.activation(quT[:, :], ps[4][0:BOT, :], ACT.Copy).then_inc(ffn_act, 1)
        act.wait_ge(ffn_mm, 2)
        act.activation(rkT[:, :], ps[5][0:RDIM, 0:NSLOT], ACT.Copy).then_inc(ffn_act, 1)
        act.wait_ge(ffn_mm, 3)
        act.activation(t1T[:, :], ps[6][0:VB, 0:NSLOT], ACT.Copy).then_inc(ffn_act, 1)
        act.wait_ge(ffn_mm, 4)
        act.activation(gl[:, 0, :], ps[0][:, :], ACT.Identity, bias=bu1[:, :]).then_inc(ffn_act, 1)
        act.wait_ge(ffn_mm, 5)
        act.activation(rqT[:, :], ps[1][0:RDIM, :], ACT.Copy).then_inc(ffn_act, 1)
        act.wait_ge(ffn_mm, 6)
        act.activation(AV[:, :], ps[2][:, :], ACT.Copy).then_inc(ffn_act, 1)
        act.wait_ge(ffn_vec, 1)
        act.activation(gl[:, 2, :], gl[:, 1, :], ACT.Tanh, scale=math.sqrt(2 / math.pi)).then_inc(ffn_act, 1)
        act.wait_ge(ffn_vec, 2)
        act.activation(gt[:, 0, :], mv2[:, :, 1], ACT.Ln, bias=1.0).then_inc(ffn_act, 1)
        act.wait_ge(ffn_vec, 4)
        act.activation(at[:, :, :], at[:, :, :], ACT.Exp).then_inc(ffn_act, 1)
        act.wait_ge(ffn_vec, 5)
        act.activation(gt[:, 4, :], gt[:, 3, :], ACT.Sigmoid).then_inc(ffn_act, 1)
        act.wait_ge(ffn_vec, 7)
        act.activation(gt[:, 8, :], gt[:, 7, :], ACT.Sigmoid).then_inc(ffn_act, 1)
        act.wait_ge(ffn_mm, 10)
        act.activation(wT[:, :, :], ps[5][:, :].rearrange("p (t k) -> p t k", t=TILES), ACT.Copy)\
           .then_inc(ffn_act, 1)

    ps_sc = ps_t[:, :].bitcast(F32)

    def attention_pe(pe):
        pe.wait_ge(fill2, 3)
        pe.wait_ge(aw_in, 16 * 7)

        def turn():
            for k in range(KC):
                for t in range(TILES):
                    ins = pe.transpose(ps[k][:, 128 * t:128 * t + 128], LN[:, t, 128 * k:128 * k + 128], ident[:, :])
                ins.then_inc(xt_mm, 1)

        pe.wait_ge(ln2_ready, 1)
        turn()
        pe.wait_ge(xt_ready, KC)
        for t in range(TILES):
            pe.matmul(ps[t][:, :], ones_row[:, :], bo[:, :], start=True, stop=False, skip_group_check=True)

        with pe.Fori(0, NGRP // 2) as h:
            for u in range(2):
                pe.wait_ge(wqkv_in[u], h * 48 + 48)
                heads = h * (2 * (REP + 1)) + u * (REP + 1)
                for j in range(REP + 1):
                    col = REP * DH if j == 0 else (j - 1) * DH
                    bank = ps[4 + j % 2]
                    if j >= 2:
                        pe.wait_ge(rope_parts, heads + (j - 1))
                    elif j == 0:
                        pe.wait_ge(ct_ready, 1 + h * (2 * TILES) + u * TILES)
                    for k in range(KC):
                        ins = pe.matmul(bank[:, :], wqkv[:, u, k, col:col + DH], XT[:, k, :],
                                        start=(k == 0), stop=(k == KC - 1))
                    ins.then_inc(proj_mm, 1)
                pe.wait_ge(pt_ready, 1 + h * 2 + u)
                col = (REP + 1) * DH
                for t in range(TILES):
                    for k in range(KC):
                        pe.matmul(ps[6][:, 128 * t:128 * t + 128], XT[:, k, 128 * t:128 * t + 128],
                                  wqkv[:, u, k, col:col + DH], start=(k == 0), stop=False)
                    ins = pe.matmul(ps[6][:, 128 * t:128 * t + 128], ones_row[:, :],
                                    bv[:, bass.ds(h * (2 * DH) + u * DH, DH)], start=False, stop=True)
                ins.then_inc(v_mm, 1)
                pe.wait_ge(qk_ready, 1 + heads + (REP + 1))
                pe.wait_ge(vt_ready, h * 2 + (u + 1))
                for b in range(B):
                    ins = pe.matmul(ps_sc[:, 32 * b:32 * b + 32], qT[:, b, :, :],
                                    kT[:, 32 * b:32 * b + 32], start=True, stop=True)
                ins.then_inc(sc_mm, 1)
                pe.wait_ge(pr_ready, h * 2 + (u + 1))
                for t in range(TILES):
                    ins = pe.transpose(ps[6][:, 128 * t:128 * t + 128], pr[:, 4 * t:4 * t + 4, :], ident[:, :])
                ins.then_inc(pt_mm, 1)
                pe.wait_ge(pt_ready, 1 + h * 2 + (u + 1))
                for t in range(TILES):
                    if t >= 2:
                        pe.wait_ge(ct_ready, 1 + h * (2 * TILES) + (u * TILES + t - 1))
                    pe.matmul(ps[4 + t % 2][:, :], vt[:, t, :], PT[:, t, :, :], start=True, stop=True)\
                      .then_inc(ctx_mm, 1)
                pe.wait_ge(wo_in[u], h * 16 + 16)
                for t in range(TILES):
                    pe.wait_ge(ct_ready, 1 + h * (2 * TILES) + (u * TILES + t + 1))
                    for r in range(REP):
                        ins = pe.matmul(ps[t][:, :], CT[:, t, r, :, :], wo[:, u, r, :], start=False, stop=False,
                                        skip_group_check=True)
                ins.then_inc(wo_used, 1)
        pe.wait_ge(fw_in, 16 * 13)
        pe.wait_ge(ln2_ready, 2)
        turn()
        pe.wait_ge(xt_ready, 2 * KC)
        for k in range(KC):
            ins = pe.matmul(ps[4][0:BOT, :], fWq[:, k, :], XT[:, k, :], start=(k == 0), stop=(k == KC - 1))
        ins.then_inc(ffn_mm, 1)
        pe.matmul(ps[5][0:RDIM, 0:NSLOT], fWr[:, :], akT[:, :], start=True, stop=True).then_inc(ffn_mm, 1)
        for k in range(KC):
            ins = pe.matmul(ps[6][0:VB, 0:NSLOT], wvd[:, k, :], avT[:, k, :], start=(k == 0), stop=(k == KC - 1))
        ins.then_inc(ffn_mm, 1)
        for k in range(KC):
            ins = pe.matmul(ps[0][:, :], wu1[:, k, :], XT[:, k, :], start=(k == 0), stop=(k == KC - 1))
        ins.then_inc(ffn_mm, 1)
        pe.wait_ge(ffn_act, 1)
        pe.matmul(ps[1][0:RDIM, :], fWr[:, :], quT[:, :], start=True, stop=True).then_inc(ffn_mm, 1)
        pe.wait_ge(ffn_act, 3)
        pe.matmul(ps[2][:, :], t1T[:, :], wvu[:, :], start=True, stop=True).then_inc(ffn_mm, 1)
        pe.wait_ge(ffn_act, 5)
        for t in range(TILES):
            ins = pe.matmul(ps[3][:, 128 * t:128 * t + 128], rqT[:, 128 * t:128 * t + 128], rkT[:, :],
                            start=True, stop=True)
        ins.then_inc(ffn_mm, 1)
        for t in range(TILES):
            ins = pe.matmul(ps[4][:, 128 * t:128 * t + 128], quT[:, 128 * t:128 * t + 128], akT[:, :],
                            start=True, stop=True)
        ins.then_inc(ffn_mm, 1)
        pe.wait_ge(ffn_vec, 3)
        pe.wait_ge(ffn_act, 8)
        pe.matmul(ps[6][:, 0:TILES], ones_sq[:, :], gt[:, 0, :], start=True, stop=True)
        for t in range(TILES):
            ins = pe.matmul(ps[6][:, 8 + t:9 + t], gl[:, 3, 128 * t:128 * t + 128], wu2[:, :], start=True, stop=True)
        ins.then_inc(ffn_mm, 1)
        pe.wait_ge(ffn_vec, 8)
        for t in range(TILES):
            ins = pe.transpose(ps[5][:, 128 * t:128 * t + 128], at[:, t, :], ident[:, :])
        ins.then_inc(ffn_mm, 1)
        pe.wait_ge(ffn_act, 12)
        for t in range(TILES):
            pe.matmul(ps[t][:, :], wT[:, t, :], AV[:, :], start=True, stop=True).then_inc(ffn_mm, 1)

    @block.tensor
    def _(pe):
        pe.wait_ge(w_in, 16 * 12)
        pe.wait_ge(consts_in, 16 * len(small))
        for L in range(2):
            oc = OUTC[L]
            if L:
                pe.wait_ge(weff_ev, 2)
            for part, off in ((0, 128), (1, 0)):
                for m in range(M):
                    mi = PERMS[L].index(m)
                    ins = pe.matmul(ps_ga[32 * m:32 * m + 32, part * 64:part * 64 + oc],
                                    Wl[L][:, off + mi:off + mi + 125:4], Wc[L][:, :], start=True, stop=True)
            ins.then_inc(weff_mm, 1)
            pe.wait_ge(w4_ready, L + 1)
            pe.matmul(ps_v[0:64, 0:oc], fold[:, :], W4[L][:, :], start=True, stop=True).then_inc(weff_mm, 1)
            pe.matmul(ps_v[64:65, 0:oc], bl[L][:, :], Wc[L][:, :], start=True, stop=True).then_inc(weff_mm, 1)
        pe.wait_ge(key_back, 64)
        for c in range(CH):
            ins = pe.transpose(ps_mt[:, 64 * c:64 * c + 64], K64[:, 128 * c:128 * c + 128], ident[0:64, 0:64])
        ins.then_inc(key_turned, 1)

        def scores(base, t):
            if t >= 2:
                pe.wait_ge(s_ready, base + (t - 1))
            for k in range(BLKS):
                at0 = (t * BLKS + k) * TOK
                for b in range(2):
                    dst = ps_ga[64 * b:64 * b + 64, (t % 2) * 256 + 32 * k:(t % 2) * 256 + 32 * k + 32]
                    for j, (l, r) in enumerate(((0, 0), (1, 0), (0, 1))):
                        ins = pe.matmul(dst, LB[:, b, l, at0:at0 + WIN, :], R[:, b, r, :, at0:at0 + WIN],
                                        start=(j == 0), stop=(j == 2))
            ins.then_inc(ga_ready, 1)

        def values(L, base, t):
            oc = OUTC[L]
            pe.wait_ge(fw_ready, base + (t + 1))
            if t >= 1:
                pe.wait_ge(vbd_ready, base + t)
            for k in range(BLKS):
                ins = pe.matmul(ps_v[:, k * oc:k * oc + oc], FW[:, t % 2, k, :], WD[L][:, :],
                                start=True, stop=True)
            ins.then_inc(v_ready, 1)

        for L in range(2):
            oc = OUTC[L]
            if L == 0:
                pe.wait_ge(zeros_done, 1)
                pe.wait_ge(weff_ev, 4)
                pe.wait_ge(kcol_ready, 1)
            with pe.Fori(0, PAIRS) as q:
                idx = q + L * PAIRS
                base = q * STEPS + L * PAIRS * STEPS
                pe.wait_ge(pair_done, 1 + idx)
                pe.wait_ge(fs_ready, idx + 1)
                pe.nop(nofuse=True)
                for c in range(CH):
                    for h in range(2):
                        o0 = (2 * c + h) * 64
                        ins = pe.transpose(ps_t[:, o0:o0 + 64], FS[:, h, 128 * c:128 * c + 128], ident_h[0:64, 0:64])
                ins.then_inc(turned, 1)
                pe.wait_ge(tt_ready, idx + 1)
                for b in range(2):
                    pe.wait_ge(onehot_ready, idx * 2 + (b + 1))
                    for h, dst in enumerate(((ps_mt, ps_mb), (ps_rb, ps_o[0]))[b]):
                        for m in range(M):
                            for c in range(CH):
                                ins = pe.matmul(dst[32 * m:32 * m + 32, :], TT[:, c, h, 32 * b:32 * b + 32],
                                                P1H[:, b, m, c, :], start=(c == 0), stop=(c == CH - 1))
                    ins.then_inc(perm_mm, 1)
                pe.wait_ge(lb_ready, idx + 1)
                pe.wait_ge(ctr_in, idx * 128 + 128)
                scores(base, 0)
                values(L, base, 0)
                for t in range(STEPS + 1):
                    if t >= 1:
                        pe.wait_ge(rze_ready, base + t)
                        if t >= 2:
                            pe.wait_ge(an_ready, base + (t - 1))
                        for j in range(4):
                            ins = pe.matmul(ps_rb[:, 120 * j:120 * j + 120], rZe[:, 128 * j:128 * j + 128], ident[0:120, 0:120],
                                            start=True, stop=True)
                        ins.then_inc(rb_ready, 1)
                    if t < STEPS:
                        pe.wait_ge(s_ready, base + (t + 1))
                        if t >= 1:
                            pe.wait_ge(mts_ready, base + t)
                        sbf = S[:, t % 2, :].bitcast(BF16)
                        for j in range(4):
                            ins = pe.matmul(ps_mt[0:120, 128 * j:128 * j + 128],
                                            sbf[:, 240 * j + 1:240 * j + 240:2], ident_bf[:, :],
                                            start=True, stop=True)
                        ins.then_inc(mt_ready, 1)
                        if t + 1 < STEPS:
                            scores(base, t + 1)
                            values(L, base, t + 1)
                        pe.wait_ge(mte_ready, base + (t + 1))
                        if t >= 1:
                            pe.wait_ge(d_ready, base + t)
                        for j in range(4):
                            ins = pe.matmul(ps_mb[:, 120 * j:120 * j + 120], MTe[:, 128 * j:128 * j + 128],
                                            ident_bf[0:120, 0:120], start=True, stop=True)
                        ins.then_inc(mb_ready, 1)
                    if t >= 1:
                        u = t - 1
                        if u >= 2:
                            pe.wait_ge(o_used, base + (u - 1))
                        dst = ps_o[u % 2]
                        pe.matmul(dst[0:2 * oc, 0:NCOL], Wcc[L][:, :],
                                  view(C2, slice(0, 65), u * STEPT, [[1, STEPT], [0, K]]), start=True, stop=False,
                                  skip_group_check=True)
                        pe.wait_ge(an_ready, base + (u + 1))
                        pe.wait_ge(vbd_ready, base + (u + 1))
                        for k in range(BLKS):
                            ins = pe.matmul(dst[0:2 * oc, 60 * k:60 * k + 60],
                                            Vbd[:, u % 2, 2 * oc * k:2 * oc * k + 2 * oc],
                                            AN[:, u % 2, 60 * k:60 * k + 60], start=False, stop=(k == BLKS - 1),
                                            skip_group_check=True)
                        ins.then_inc(o_ready, 1)
                    if t < STEPS:
                        pe.wait_ge(e_ready, base + (t + 1))
                        if t >= 1:
                            pe.wait_ge(rz_ready, base + t)
                        for j in range(4):
                            ins = pe.matmul(ps_rb[0:120, 480 + 8 * j:488 + 8 * j], A[:, t % 2, 120 * j:120 * j + 120],
                                            group8[:, :], start=True, stop=True)
                        ins.then_inc(z_ready, 1)
                if L == 1:
                    pe.wait_ge(f2_ready, q * 2 + 1)
                    pe.nop(nofuse=True)
                    pe.matmul(ps_ga[0:64, :], W3a[:, :], fy[0:64, :], start=True, stop=False)
                    pe.matmul(ps_ga[0:64, :], W3b[:, :], C2[0:64, 0:N], start=False, stop=False)
                    pe.matmul(ps_ga[0:64, :], W3c[:, :], F2[:, :], start=False, stop=True).then_inc(h3_mm, 1)
        attention_pe(pe)


    @block.vector
    def _(v):
        o = Order(v, vec)
        v.wait_ge(coord_in, 48)
        o.did(v.tensor_reduce(cs[:, 0:1], coord[:, :], AX, ALU.max))
        o.did(v.tensor_reduce(cs[:, 1:2], coord[:, :], AX, ALU.min))
        o.sync()
        o.step(v.tensor_tensor(cs[:, 2:3], cs[:, 0:1], cs[:, 1:2], ALU.subtract))
        o.step(v.tensor_scalar(cs[:, 3:4], cs[:, 2:3], 1e-6, None, ALU.add))
        o.step(v.reciprocal(cs[:, 4:5], cs[:, 3:4]))
        o.step(v.tensor_scalar(cs[:, 5:6], cs[:, 4:5], float(2 ** BITS - 1), None, ALU.mult))
        o.step(v.tensor_scalar(qf[:, 0, :], coord[:, :], cs[:, 1:2], cs[:, 5:6], ALU.subtract, ALU.mult))
        o.step(v.tensor_copy(qi[:, :], qf[:, 0, :]))
        o.step(v.tensor_copy(qf[:, 1, :], qi[:, :]))
        o.step(v.tensor_tensor(qf[:, 2, :], qf[:, 1, :], qf[:, 0, :], ALU.is_gt))
        o.step(v.tensor_tensor(qf[:, 1, :], qf[:, 1, :], qf[:, 2, :], ALU.subtract))
        o.step(v.tensor_scalar(qf[:, 1, :], qf[:, 1, :], 0.0, float(2 ** BITS - 1), ALU.max, ALU.min))
        v.tensor_copy(qi[:, :], qf[:, 1, :]).then_inc(q_ready, 1)
        v.wait_ge(q_back, 16)

        def interleave(x):
            for s, mask in ((16, 0x030000FF), (8, 0x0300F00F), (4, 0x030C30C3), (2, 0x09249249)):
                o.step(v.tensor_scalar(SP1[:, :, :, :], x, s, None, ALU.logical_shift_left))
                o.step(v.tensor_tensor(x, x, SP1[:, :, :, :], ALU.bitwise_or))
                o.step(v.tensor_scalar(x, x, mask, None, ALU.bitwise_and))

        for j in range(3):
            for w, src in enumerate((j, (1, 0, 2)[j])):
                o.did(v.tensor_copy(HX[:, j, w, :], XQ[:, src, :]))
        o.sync()
        h = [HX[:, j, :, :] for j in range(3)]
        msk, dif, tmp, acc = [hm[:, j, :, :] for j in range(4)]

        def bit_mask(dst, src, bit):
            o.step(v.tensor_scalar(dst, src, 31 - bit, None, ALU.logical_shift_left))
            o.step(v.tensor_scalar(dst, dst, 31, None, ALU.arith_shift_right))

        for bit in range(BITS - 1, 0, -1):
            low = (1 << bit) - 1
            bit_mask(msk, h[0], bit)
            o.step(v.tensor_scalar(msk, msk, low, None, ALU.bitwise_and))
            o.step(v.tensor_tensor(h[0], h[0], msk, ALU.bitwise_xor))
            for j in (1, 2):
                bit_mask(msk, h[j], bit)
                o.step(v.tensor_tensor(dif, h[0], h[j], ALU.bitwise_xor))
                o.step(v.tensor_tensor(dif, dif, msk, ALU.bitwise_or))
                o.step(v.tensor_scalar(tmp, dif, low, None, ALU.bitwise_and))
                o.step(v.tensor_tensor(h[0], h[0], tmp, ALU.bitwise_xor))
                o.step(v.tensor_tensor(dif, dif, msk, ALU.bitwise_xor))
                o.step(v.tensor_scalar(tmp, dif, low, None, ALU.bitwise_and))
                o.step(v.tensor_tensor(h[j], h[j], tmp, ALU.bitwise_xor))
        o.step(v.tensor_tensor(h[1], h[1], h[0], ALU.bitwise_xor))
        o.step(v.tensor_tensor(h[2], h[2], h[1], ALU.bitwise_xor))
        for n, bit in enumerate(range(BITS - 1, 0, -1)):
            low = (1 << bit) - 1
            bit_mask(msk, h[2], bit)
            dst = acc if n == 0 else tmp
            o.step(v.tensor_scalar(dst, msk, low, None, ALU.bitwise_and))
            if n:
                o.step(v.tensor_tensor(acc, acc, tmp, ALU.bitwise_xor))
        for j in range(3):
            o.did(v.tensor_tensor(h[j], h[j], acc, ALU.bitwise_xor))
        o.sync()
        for j in range(3):
            o.did(v.tensor_copy(XS[:, j, 0, :], XQ[:, j, :]))
            o.did(v.tensor_copy(XS[:, j, 1:3, :], HX[:, j, :, :]))
        o.sync()
        interleave(XS[:, :, :, :])
        for m, (w, order) in enumerate(((0, (0, 1, 2)), (0, (1, 0, 2)), (1, (0, 1, 2)), (2, (0, 1, 2)))):
            a, b_, c_ = [XS[:, j, w, :] for j in order]
            o.did(v.tensor_scalar(KEY[:, m, :], a, 2, None, ALU.logical_shift_left))
            o.did(v.tensor_scalar(KEYT[:, m, :], b_, 1, None, ALU.logical_shift_left))
            o.sync()
            o.step(v.tensor_tensor(KEY[:, m, :], KEY[:, m, :], KEYT[:, m, :], ALU.bitwise_or))
            o.step(v.tensor_tensor(KEY[:, m, :], KEY[:, m, :], c_, ALU.bitwise_or))
        o.step(v.tensor_scalar(KEYT[:, :, :], KEY[:, :, :], 1 << 29, None, ALU.bitwise_and))
        o.step(v.tensor_scalar(KEYT[:, :, :], KEYT[:, :, :], 1, None, ALU.logical_shift_left))
        o.step(v.tensor_scalar(KEY[:, :, :], KEY[:, :, :], 1 << 29, None, ALU.bitwise_xor))
        v.tensor_tensor(KEY[:, :, :], KEY[:, :, :], KEYT[:, :, :], ALU.bitwise_or).then_inc(key_ready, 1)

        for L in range(2):
            oc = OUTC[L]
            v.wait_ge(weff_mm, 3 * L + 1)
            v.wait_ge(weff_ev, 2 * L + 1)
            v.tensor_tensor(W4[L][:, :], ps_ga[:, 64:64 + oc], WD[L][:, :], ALU.subtract).then_inc(w4_ready, 1)

        v.wait_ge(x_in, 16)
        for q in range(PAIRS):
            o.did(v.bn_stats(stx[:, q, :], X[:, q, :]))
        o.sync()
        for q in range(PAIRS):
            ins = v.bn_aggr(mv[0:64, q, :], stx[:, q, :])
        ins.then_inc(ln_var, 1)
        v.wait_ge(ln_std, 1)
        o.step(v.reciprocal(rs[0:64, :, 1], rs[0:64, :, 0]))
        for q in range(PAIRS):
            o.did(v.tensor_scalar(F0[:, q, :], X[:, q, :], mv[0:64, q, 0:1], rs[0:64, q, 1:2],
                                  ALU.subtract, ALU.mult))
        o.sync()

        v.wait_ge(kcol_ready, 1)
        v.wait_ge(zeros_done, 1)
        kview = kcol[:, :, :].rearrange("p c (m b) -> p c m b", m=M)
        with v.Fori(0, B // 2) as hb:
            for u in range(2):
                v.wait_ge(kb_in[u], hb * 16 + 16)
                b = hb * 2 + u
                v.tensor_copy(kc_b[:, :, :], kview[:, :, :, bass.ds(b, 1)].rearrange("p c m b -> p m (c b)"))\
                 .then_inc(kc_ready, 1)
                v.wait_ge(kc_ready, b + 1)
                n = 0
                for m in range(M):
                    for c in range(CH):
                        key = kc_b[:, m, c:c + 1]
                        j = m * CH + c
                        row = kb_ring[:, u, m, :]
                        for kind in range(3):
                            if kind == 0 and c == 0:
                                continue
                            if n >= 4:
                                v.wait_ge(compared, b * COMPARES + (n - 3))
                            if kind == 0:
                                ins = v.tensor_scalar(cmp[:, n % 4, 0:128 * c], row[:, 0:128 * c], key, None,
                                                      ALU.is_le, ALU.add, accum_out=cnt[:, 0, j:j + 1])
                            elif kind == 1:
                                ins = v.tensor_scalar(cmp[:, n % 4, 128 * c:N], row[:, 128 * c:N], key, None,
                                                      ALU.is_lt, ALU.add, accum_out=cnt[:, 1, j:j + 1])
                            else:
                                ins = v.scalar_tensor_tensor(out=cmp[:, n % 4, 0:128],
                                                             in0=row[:, 128 * c:128 * c + 128], scalar=key,
                                                             in1=tri[:, :], op0=ALU.is_equal, op1=ALU.mult,
                                                             accum_out=cnt[:, 2, j:j + 1])
                            ins.then_inc(compared, 1)
                            n += 1
                v.wait_ge(compared, b * COMPARES + COMPARES)
                v.tensor_tensor(cnt[:, 1, :], cnt[:, 1, :], cnt[:, 2, :], ALU.add).then_inc(kb_used, 1)
                v.wait_ge(kb_used, 1 + b + 1)
                v.tensor_tensor(rank[:, bass.ds(b, 1), :].rearrange("p a k -> p (a k)"), cnt[:, 0, :], cnt[:, 1, :],
                                ALU.add).then_inc(rank_ready, 1)
                v.wait_ge(rank_ready, b + 1)

        def logits(base, t):
            half = (t % 2) * 256
            v.wait_ge(ga_ready, base + (t + 1))
            kind = 0 if t == 0 else 1
            g = ps_ga[:, half:half + 256]
            ctr = view(ps_ga, slice(0, 128), half + WIN, [[32, BLKS], [1, TOK]])
            v.tensor_tensor(aM[:, :].rearrange("p (k n) -> p k n", k=BLKS), ctr,
                            keymask[:, kind * STEPT:kind * STEPT + STEPT].rearrange("p (k n) -> p k n", k=BLKS),
                            ALU.add).then_inc(am_ready, 1)

        def logits2(base, t):
            half = (t % 2) * 256
            v.wait_ge(am_ready, base + (t + 1))
            if t >= 2:
                v.wait_ge(e_ready, base + (t - 1))
            so = (t % 2) * NCOL

            def part(k0, nk, n0, nn, i0, ni, q0, qn, qi):
                return v.tensor_tensor(
                    view(S, slice(0, 128), so + (k0 * TOK + n0) * K + i0, [[TOK * K, nk], [K, nn], [1, ni]]),
                    view(ps_ga, slice(0, 128), half + 32 * k0 + q0, [[32, nk], [qn, nn], [qi, ni]]),
                    view(aM, slice(0, 128), k0 * TOK + n0, [[TOK, nk], [1, nn], [0, ni]]), ALU.subtract)

            if t == 0:
                for n in range(5):
                    part(0, 1, n, 1, 0, n + 6 if n < 4 else K, PADL, 1, 1)
                    if n < 4:
                        part(0, 1, n, 1, n + 6, 4 - n, PADL + n + 5, 1, 0)
                part(0, 1, 5, 1, 0, K, 5, 1, 1)
                ins = part(1, BLKS - 1, 0, TOK, 0, K, 0, 1, 1)
            else:
                ins = part(0, BLKS, 0, TOK, 0, K, 0, 1, 1)
            ins.then_inc(s_ready, 1)

        for L in range(2):
            oc = OUTC[L]
            rows = 2 * oc
            if L == 0:
                v.wait_ge(rank_ready, B)
                v.wait_ge(weff_ev, 4)
            with v.Fori(0, PAIRS) as q:
                idx = q + L * PAIRS
                base = q * STEPS + L * PAIRS * STEPS
                src = (F0, F1)[L]
                v.tensor_copy(C2[0:64, 0:N], src[:, bass.ds(q, 1), :].rearrange("p a n -> p (a n)"))\
                 .then_inc(prep, 1)
                v.tensor_copy(rank_p[:, :, :], rank[:, bass.ds(q * 2, 2), :]).then_inc(prep, 1)
                v.wait_ge(prep, idx * PREP + 2)
                v.tensor_copy(FS[:, 0, :], C2[0:64, 0:N]).then_inc(prep, 1)
                v.wait_ge(prep, idx * PREP + 3)
                v.tensor_tensor(FS[:, 1, :], C2[0:64, 0:N], FS[:, 0, :], ALU.subtract).then_inc(fs_ready, 1)
                for b in range(2):
                    for m in range(M):
                        for c in range(CH):
                            j = m * CH + c
                            ins = v.tensor_scalar(P1H[:, b, m, c, :], iota[:, :], rank_p[:, b, j:j + 1], None,
                                                  ALU.is_equal)
                    ins.then_inc(onehot_ready, 1)
                for b in range(2):
                    v.wait_ge(perm_ev, idx * 4 + (2 * b + 2))
                    for p0, p1, from_ in ((0, PADL, PADL), (PADL + N, POSW, PADL + N - 1)):
                        ins = v.tensor_copy(R[:, b, :, 0, p0:p1],
                                      view(R, slice(0, 128), b * 4 * POSW + from_, [[2 * POSW, 2], [0, p1 - p0]]))
                    ins.then_inc(pad_ready, 1)
                for t in range(STEPS + 2):
                    if t < STEPS:
                        logits(base, t)
                    if 1 <= t <= STEPS:
                        u = t - 1
                        v.wait_ge(z_ready, base + (u + 1))
                        if u >= 1:
                            v.wait_ge(rze_ready, base + u)
                        v.reciprocal(rZ[:, :], ps_rb[0:120, 480:512]).then_inc(rz_ready, 1)
                    if t < STEPS:
                        logits2(base, t)
                    if 1 <= t <= STEPS:
                        v.wait_ge(rb_ready, base + (u + 1))
                        if u >= 2:
                            v.wait_ge(o_ready, base + (u - 1))
                        v.tensor_tensor(AN[:, u % 2, :], ps_rb[:, 0:NCOL], A[:, u % 2, :], ALU.mult)\
                         .then_inc(an_ready, 1)
                    if t < STEPS:
                        v.wait_ge(mt_ready, base + (t + 1))
                        if t >= 1:
                            v.wait_ge(mte_ready, base + t)
                        v.tensor_reduce(view(MTs, slice(0, 120), 0, [[HG, 8], [1, HG]]),
                                        view(ps_mt, slice(0, 120), 0, [[HG * WIN, 8], [1, HG], [HG, WIN]]), AX, ALU.max)\
                         .then_inc(mts_ready, 1)
                    if t >= 2:
                        w = t - 2
                        v.wait_ge(o_ready, base + (w + 1))
                        v.tensor_reduce(raw[0:rows, w * STEPT:w * STEPT + STEPT],
                                        ps_o[w % 2][0:rows, 0:NCOL].rearrange("p (n i) -> p n i", i=K), AX, ALU.max)
                    if t < STEPS:
                        v.wait_ge(mb_ready, base + (t + 1))
                        v.tensor_tensor(S[:, t % 2, :], S[:, t % 2, :], ps_mb[:, 0:NCOL], ALU.subtract)\
                         .then_inc(d_ready, 1)
                    if t >= 2:
                        real = STEPT if w < STEPS - 1 else LASTT
                        v.bn_stats(st[0:rows, w, :], ps_o[w % 2][0:rows, 0:real * K]).then_inc(o_used, 1)
                v.wait_ge(o_used, base + STEPS)
                v.nop(nofuse=True)
                v.bn_aggr(mv[0:rows, 0, :], st[0:rows, :, :].rearrange("p s k -> p (s k)")).then_inc(var_ready, 1)
                v.wait_ge(std_ready, idx + 1)
                v.reciprocal(rs[0:rows, 0, 1:2], rs[0:rows, 0, 0:1]).then_inc(fin, 1)
                v.wait_ge(fin, idx * 2 + 1)
                v.tensor_scalar(fy[0:rows, :], raw[0:rows, 0:N], mv[0:rows, 0, 0:1], rs[0:rows, 0, 1:2],
                                ALU.subtract, ALU.mult).then_inc(fin, 1)
                v.wait_ge(fin, idx * 2 + 2)
                if L == 0:
                    v.scalar_tensor_tensor(out=F1[:, bass.ds(q, 1), :].rearrange("p a n -> p (a n)"),
                                           in0=fy[0:rows, :], scalar=0.2, in1=fy[0:rows, :],
                                           op0=ALU.mult, op1=ALU.max).then_inc(pair_done, 1)
                    v.wait_ge(pair_done, 1 + idx + 1)
                else:
                    v.scalar_tensor_tensor(out=F2[:, :], in0=fy[:, :], scalar=0.2, in1=fy[:, :],
                                           op0=ALU.mult, op1=ALU.max).then_inc(tail, 1)
                    v.wait_ge(tail, q * TAIL + 1)
                    v.tensor_copy(fy[0:64, :], F0[:, bass.ds(q, 1), :].rearrange("p a n -> p (a n)"))\
                     .then_inc(f2_ready, 1)
                    v.wait_ge(h3_mm, q + 1)
                    v.bn_stats(st[0:64, 0, :], ps_ga[0:64, :]).then_inc(tail, 1)
                    v.wait_ge(tail, q * TAIL + 2)
                    v.nop(nofuse=True)
                    v.bn_aggr(mv[0:64, 1, :], st[0:64, 0, :]).then_inc(f2_ready, 1)
                    v.wait_ge(ln_std, q + 2)
                    v.reciprocal(rs[0:64, 1, 1:2], rs[0:64, 1, 0:1]).then_inc(tail, 1)
                    v.wait_ge(tail, q * TAIL + 3)
                    v.tensor_scalar(h3[:, :], ps_ga[0:64, :], mv[0:64, 1, 0:1], rs[0:64, 1, 1:2],
                                    ALU.subtract, ALU.mult).then_inc(tail, 1)
                    v.wait_ge(tail, q * TAIL + 4)
                    v.scalar_tensor_tensor(out=fy[0:64, :], in0=h3[:, :], scalar=0.2, in1=h3[:, :],
                                           op0=ALU.mult, op1=ALU.max).then_inc(tail, 1)
                    v.wait_ge(tail, q * TAIL + 5)
                    xq = X[:, bass.ds(q, 1), :].rearrange("p a n -> p (a n)")
                    v.tensor_tensor(xq, xq, fy[0:64, :], ALU.add).then_inc(pair_done, 1)
                    v.wait_ge(pair_done, 1 + idx + 1)
        v.memset(C2[0:1, 0:1], 0.0).then_inc(graph_done, 1)

        def layernorm(n):
            for t in range(TILES):
                o.did(v.bn_stats(st2[:, t, :], XN[:, t, :]))
            o.sync()
            for t in range(TILES):
                ins = v.bn_aggr(mv2[:, t, :], st2[:, t, :])
            ins.then_inc(ln2_var, 1)
            v.wait_ge(ln2_std, n)
            o.step(v.reciprocal(rs2[:, :, 1], rs2[:, :, 0]))
            for t in range(TILES):
                ins = v.tensor_scalar(LN[:, t, :], XN[:, t, :], mv2[:, t, 0:1], rs2[:, t, 1:2],
                                      ALU.subtract, ALU.mult)
            ins.then_inc(ln2_ready, 1)

        v.wait_ge(graph_done, 1)
        v.wait_ge(xn_in, 32)
        layernorm(1)
        v.wait_ge(aw_in, 16 * 7)
        pos = lambda r: view(cosT, r, 0, [[0, B], [1, C]])
        snv = lambda r: view(sinT, r, 0, [[0, B], [1, C]])
        by_b = lambda a: a.rearrange("p (b s) -> p b s", b=B)
        with v.Fori(0, NGRP) as g:
            for j in range(REP + 1):
                if j == 0:
                    v.tensor_copy(bg[:, 0:1], bk[:, bass.ds(g, 1)]).then_inc(bg_ready, 1)
                    v.tensor_copy(bg[:, 1:REP + 1], bq[:, bass.ds(g * REP, REP)]).then_inc(bg_ready, 1)
                    v.wait_ge(bg_ready, g * 2 + 2)
                bank = ps[4 + j % 2]
                v.wait_ge(proj_mm, g * (REP + 1) + (j + 1))
                if j >= 2:
                    v.wait_ge(qk_ready, 1 + g * (REP + 1) + (j - 1))
                else:
                    v.wait_ge(qk_ready, 1 + g * (REP + 1))
                v.scalar_tensor_tensor(out=by_b(r1[:, j % 2, :]), in0=by_b(bank[:, :]), scalar=bg[:, j:j + 1],
                                       in1=pos(slice(0, 128)), op0=ALU.add, op1=ALU.mult)
                v.scalar_tensor_tensor(out=by_b(r2[0:64, j % 2, :]), in0=by_b(bank[64:128, :]),
                                       scalar=bg[64:128, j:j + 1], in1=snv(slice(64, 128)),
                                       op0=ALU.add, op1=ALU.mult)
                v.scalar_tensor_tensor(out=by_b(r2[64:128, j % 2, :]), in0=by_b(bank[0:64, :]),
                                       scalar=bg[0:64, j:j + 1], in1=snv(slice(0, 64)),
                                       op0=ALU.add, op1=ALU.mult).then_inc(rope_parts, 1)
            v.wait_ge(sc_mm, 1 + g + 1)
            v.scalar_tensor_tensor(out=pr[:, :, :], in0=by_b(ps_sc[:, :]), scalar=1.0 / math.sqrt(DH),
                                   in1=view(causal, slice(0, 128), 0, [[0, B], [1, C]]), op0=ALU.mult, op1=ALU.add)\
             .then_inc(soft, 1)
            v.wait_ge(soft, g * SOFT + 1)
            v.tensor_reduce(pm[:, 0, :], pr[:, :, :], AX, ALU.max).then_inc(soft, 1)
            v.wait_ge(soft, g * SOFT + 2)
            v.tensor_tensor(pr[:, :, :], pr[:, :, :], view(pm, slice(0, 128), 0, [[1, B], [0, C]]), ALU.subtract)\
             .then_inc(sm_ready, 1)
            v.wait_ge(ex_ready, g + 1)
            v.tensor_reduce(pm[:, 1, :], pr[:, :, :], AX, ALU.add).then_inc(soft, 1)
            v.wait_ge(soft, g * SOFT + 3)
            v.reciprocal(pm[:, 2, :], pm[:, 1, :]).then_inc(soft, 1)
            v.wait_ge(soft, g * SOFT + 4)
            v.tensor_tensor(pr[:, :, :], pr[:, :, :], view(pm, slice(0, 128), 2 * B, [[1, B], [0, C]]), ALU.mult)\
             .then_inc(pr_ready, 1)
        v.wait_ge(wo_used, 1 + NGRP)
        for t in range(TILES):
            o.did(v.tensor_tensor(XN[:, t, :], ps[t][:, :], XN[:, t, :], ALU.add))
        o.sync()
        layernorm(2)

        def did(ins):
            ins.then_inc(ffn_vec, 1)

        v.wait_ge(ln2_ready, 2)
        for t in range(TILES):
            o.did(v.bn_stats(st2[:, t, :], LN[:, t, :]))
        o.sync()
        v.wait_ge(ffn_act, 4)
        o.step(v.tensor_tensor(gl[:, 1, :], gl[:, 0, :], gl[:, 0, :], ALU.mult))
        o.step(v.tensor_scalar(gl[:, 1, :], gl[:, 1, :], 0.044715, 1.0, ALU.mult, ALU.add))
        did(v.tensor_tensor(gl[:, 1, :], gl[:, 1, :], gl[:, 0, :], ALU.mult))
        for t in range(TILES):
            ins = v.bn_aggr(mv2[:, t, :], st2[:, t, :])
        did(ins)
        v.wait_ge(ffn_act, 7)
        o.step(v.tensor_scalar(gl[:, 2, :], gl[:, 2, :], 1.0, 0.5, ALU.add, ALU.mult))
        did(v.tensor_tensor(gl[:, 3, :], gl[:, 2, :], gl[:, 0, :], ALU.mult))
        v.wait_ge(ffn_mm, 8)
        v.wait_ge(fw_in, 16 * 13)
        lr = view(lrel, slice(0, 128), 0, [[0, TILES], [1, NSLOT]])
        by_t = lambda a: a.rearrange("p (t k) -> p t k", t=TILES)
        o.did(v.scalar_tensor_tensor(out=rt[:, :, :], in0=by_t(ps[3][:, :]), scalar=1.0 / math.sqrt(RDIM), in1=lr,
                                     op0=ALU.mult, op1=ALU.add))
        o.did(v.scalar_tensor_tensor(out=at[:, :, :], in0=by_t(ps[4][:, :]), scalar=1.0 / math.sqrt(BOT), in1=lr,
                                     op0=ALU.mult, op1=ALU.add))
        o.sync()
        for t in range(TILES):
            o.did(v.max(top[:, t, :], rt[:, t, :]))
        o.sync()
        for t in range(TILES):
            o.did(v.match_replace(rp[:, t, :], top[:, t, :], rt[:, t, :], -3e38))
        o.sync()
        o.step(v.tensor_tensor(rp[:, :, :], rp[:, :, :], rt[:, :, :], ALU.is_equal))
        o.step(v.scalar_tensor_tensor(out=at[:, :, :], in0=rp[:, :, :], scalar=-1e30, in1=at[:, :, :],
                                      op0=ALU.mult, op1=ALU.add))
        o.step(v.tensor_reduce(gt[:, 1, :], at[:, :, :], AX, ALU.max))
        did(v.tensor_tensor(at[:, :, :], at[:, :, :], view(gt, slice(0, 128), 1 * TILES, [[1, TILES], [0, NSLOT]]),
                            ALU.subtract))
        v.wait_ge(ffn_mm, 9)
        did(v.tensor_scalar(gt[:, 3, :], ps[6][:, 8:8 + TILES], sc3[:, 0:1], None, ALU.add))
        o.step(v.tensor_reduce(gt[:, 2, 0:1], ps[6][:, 0:TILES], AX, ALU.add))
        o.step(v.tensor_scalar(gt[:, 2, 1:2], gt[:, 2, 0:1], 1.0 / TOKENS, 1e-6, ALU.mult, ALU.add))
        o.step(v.reciprocal(gt[:, 2, 2:3], gt[:, 2, 1:2]))
        o.step(v.tensor_scalar(gt[:, 5, :], gt[:, 0, :], gt[:, 2, 2:3], 0.5, ALU.mult, ALU.mult))
        v.wait_ge(ffn_act, 10)
        o.step(v.scalar_tensor_tensor(out=gt[:, 5, :], in0=gt[:, 4, :], scalar=2.5, in1=gt[:, 5, :],
                                      op0=ALU.mult, op1=ALU.add))
        o.step(v.tensor_scalar(gt[:, 5, :], gt[:, 5, :], 0.0, 5.0, ALU.max, ALU.min))
        o.step(v.tensor_scalar(gt[:, 5, :], gt[:, 5, :], 0.5, 1.0 / 1.5, ALU.subtract, ALU.mult))
        o.step(v.tensor_scalar(gt[:, 5, :], gt[:, 5, :], 0.0, 1.0, ALU.max, ALU.min))
        did(v.tensor_scalar(gt[:, 6, :], gt[:, 5, :], 0.0, None, ALU.add))
        v.wait_ge(ffn_vec, 6)
        did(v.tensor_scalar(gt[:, 7, :], gt[:, 5, :], sc3[:, 1:2], sc3[:, 2:3], ALU.mult, ALU.add))
        v.wait_ge(ffn_act, 9)
        o.step(v.tensor_reduce(gt[:, 9, :], at[:, :, :], AX, ALU.add))
        o.step(v.reciprocal(gt[:, 10, :], gt[:, 9, :]))
        did(v.tensor_tensor(at[:, :, :], at[:, :, :], view(gt, slice(0, 128), 10 * TILES, [[1, TILES], [0, NSLOT]]),
                            ALU.mult))
        v.wait_ge(ffn_act, 11)
        o.step(v.tensor_scalar(gt[:, 6, :], gt[:, 8, :], 0.05, None, ALU.is_ge))
        o.step(v.tensor_tensor(gt[:, 11, :], gt[:, 8, :], gt[:, 6, :], ALU.mult))
        for t in range(TILES):
            o.did(v.tensor_tensor(XN[:, t, :], XN[:, t, :], LN[:, t, :], ALU.add))
        o.sync()
        for t in range(TILES):
            v.wait_ge(ffn_mm, 11 + t)
            ins = v.scalar_tensor_tensor(out=XN[:, t, :], in0=ps[t][:, :], scalar=gt[:, 11, t:t + 1],
                                         in1=XN[:, t, :], op0=ALU.mult, op1=ALU.add)
            ins.then_inc(row_ready, 1)

    ctx.close()


def kernel(**inputs):
    import numpy as _np
    import concourse.bacc as _bacc
    from concourse import mybir as _mybir
    from concourse.bass_utils import run_bass_kernel_spmd as _run

    a = {n: _np.asarray(x) for n, x in inputs.items()}
    pre, att, ffn = "L0_xattn_", "L0_attn_", "L0_ffn_"
    data = {
        "x": a["x"], "ctx_4096": a["ctx_4096"],
        "wlin0": a[pre + "W_lin1"], "wlin1": a[pre + "W_lin2"],
        "wconv0T": a[pre + "W_conv1"].T, "wconv1T": a[pre + "W_conv2"].T, "wconv3T": a[pre + "W_conv3"].T,
        "blin0": a[pre + "b_lin1"], "blin1": a[pre + "b_lin2"],
        "Wq": a[att + "Wq"], "Wk": a[att + "Wk"], "Wv": a[att + "Wv"], "Wo": a[att + "Wo"],
        "bqT": a[att + "bq"].reshape(NHEAD, DH).T, "bkT": a[att + "bk"].reshape(NGRP, DH).T,
        "bv": a[att + "bv"], "bo": a[att + "bo"],
        "fWqT": a[ffn + "Wq"].T, "WrT": a[ffn + "Wr"].T, "akT": a[ffn + "aux_keys"].T,
        "avT": a[ffn + "aux_values"].T, "WvdT": a[ffn + "Wvd"].T, "WvuT": a[ffn + "Wvu"].T,
        "Wu1T": a[ffn + "Wu1"].T, "bu1": a[ffn + "bu1"], "Wu2T": a[ffn + "Wu2"].T, "bu2": a[ffn + "bu2"],
        "gate_w1": a[ffn + "gate_w1"].reshape(1), "gate_bias": a[ffn + "gate_bias"].reshape(1),
        "log_rel": a[ffn + "log_rel"],
    }
    data.update(constants())
    nc = _bacc.Bacc("TRN2", target_bir_lowering=False, num_devices=1)
    arrays, io = {}, {}
    for name, v in data.items():
        v = _np.ascontiguousarray(v)
        arrays[f"in_{name}"] = v
        io[name] = nc.dram_tensor(f"in_{name}", v.shape, _mybir.dt.from_np(v.dtype), kind="ExternalInput").ap()
    out = nc.dram_tensor("out_0", (B, C, N), _mybir.dt.float32, kind="ExternalOutput").ap()
    build(nc, io, out)
    r = _run(nc, [arrays], core_ids=[0])
    return r.results[0]["out_0"]
```

```python
import math
from contextlib import ExitStack

import numpy as np
import concourse.bass as bass
from concourse import mybir

F32 = mybir.dt.float32
F16 = mybir.dt.float16
BF16 = mybir.dt.bfloat16
I32 = mybir.dt.int32
ALU = mybir.AluOpType
ACT = mybir.ActivationFunctionType
AX = mybir.AxisListType.X

B, C, N = 16, 32, 512
M = 4
K = 10
BITS = 10
HD = 32
EPS = 1e-5
EXP_LN_SET = 6
PERMS = ([2, 0, 3, 1], [1, 3, 0, 2])
OUTC = (32, 64)

PAIRS = B // 2
WIN = 16
TOK = 6
BLKS = 8
STEPT = BLKS * TOK
STEPS = -(-N // STEPT)
NCOL = STEPT * K
LASTT = N - (STEPS - 1) * STEPT
PADL = 5
POSW = 544
HG = 4
CH = N // 128
TW = STEPS * STEPT
CHUNKS = -(-STEPS // 2)
VCH = [128, 128, 128, 128, POSW - 512]
VUNITS = ([[(0, 0), (0, 1), (0, 2), (0, 3)], [(1, 0), (1, 1), (1, 2), (1, 3)], [(0, 4), (1, 4)]],
          [[(0, 0), (0, 1)], [(0, 2), (0, 3)], [(1, 0), (1, 1)], [(1, 2), (1, 3)], [(0, 4), (1, 4)]])
VFIRST = (2, 3)

NHEAD, NGRP, DH = 32, 8, 128
REP = NHEAD // NGRP
HID = 512
TOKENS = B * C
TILES = TOKENS // 128
KC = HID // 128

BOT, RDIM, NSLOT, VB = 64, 48, 128, 32


def constants():
    t = {}
    t["iota"] = np.broadcast_to(np.arange(N, dtype=np.float16), (128, N)).copy()
    p = np.arange(128)
    t["ident"] = np.eye(128, dtype=np.float32)
    t["headmask"] = ((p[:, None] % 32) // 8 == np.arange(4)[None, :]).astype(np.float32)
    t["tri"] = (np.arange(128)[None, :] < p[:, None]).astype(np.float32)
    group = p // 64 * 4 + p % 4
    t["group"] = (group[:, None] == group[None, :]).astype(np.float32)
    t["fold"] = (p[:, None] % 32 == np.arange(128)[None, :] % 32).astype(np.float32)
    w = p % 64 // HG
    blk, nl = np.arange(STEPT) // TOK, np.arange(STEPT) % TOK
    ok = (w[:, None] >= nl[None, :]) & (w[:, None] < nl[None, :] + K)
    std = np.where(ok, 0.0, 1e30).astype(np.float32)
    first = std.copy()
    for n in range(5):
        pos = w - PADL
        first[:, n] = np.where((pos >= 0) & (pos <= n + 5), 0.0, 1e30)
        first[pos == n + 5, n] = -math.log(5 - n) * math.sqrt(HD)
    t["keymask"] = np.stack([first, std], 1).reshape(128, 2 * STEPT).astype(np.float32)
    half = DH // 2
    inv = (1.0 / 10000.0 ** (np.arange(half, dtype=np.float32) / np.float32(half))).astype(np.float32)
    ang = np.arange(C, dtype=np.float32)[None, :] * inv[:, None]
    cos, sin = np.cos(ang).astype(np.float32), np.sin(ang).astype(np.float32)
    t["cos"] = np.concatenate([cos, cos], 0)
    t["sin"] = np.concatenate([sin, -sin], 0)
    s = p % 32
    t["causal"] = np.where(np.arange(32)[None, :] <= s[:, None], 0.0, -1e30).astype(np.float32)
    return t


def build(nc, io, out):
    ctx = ExitStack()

    def sb(name, shape, dt, c=ctx):
        return c.enter_context(nc.sbuf_tensor(name, shape, dt))

    def sem(name):
        return ctx.enter_context(nc.semaphore(name))

    def view(tensor, rows, offset, dims):
        a = tensor[rows, ...] if not isinstance(rows, slice) else tensor[rows]
        return bass.AP(tensor=a.tensor, offset=a.offset + offset, ap=[list(a.ap[0])] + [list(d) for d in dims])

    ps = [ctx.enter_context(nc.psum_tensor(f"bank{i}", [128, 512], F32)) for i in range(7)]
    ps_t = ctx.enter_context(nc.psum_tensor("bank_t", [128, 1024], F16))
    ps_ga, ps_p, ps_mt, ps_mb, ps_z = ps[0:5]
    ps_o = ps[5:7]
    ps_t32 = ps_t[:, :].bitcast(F32)

    iota = sb("iota", [128, N], F16)
    ident = sb("ident", [128, 128], F32)
    ident_bf = sb("ident_bf", [128, 128], BF16)
    ident_h = sb("ident_h", [128, 128], F16)
    headmask = sb("headmask", [128, 4], F32)
    tri = sb("tri", [128, 128], F32)
    group = sb("group", [128, 128], F32)
    fold = sb("fold", [128, 128], F32)
    keymask = sb("keymask", [128, 2 * STEPT], F32)
    eps_col = sb("eps_col", [128, 1], F32)
    started = sb("started", [128, 9], F32)
    small = {n: t for n, t in (("iota", iota), ("ident", ident), ("headmask", headmask), ("tri", tri),
                               ("group", group), ("fold", fold), ("keymask", keymask))}
    FF = sb("FF", [64, 2 * PAIRS + 1, N], F32)

    g1 = ExitStack()
    rank = sb("rank", [128, 2 * B + 4, M * CH], F32, g1)
    rank_p = sb("rank_p", [128, 2, M * CH], F32, g1)
    kcol = sb("kcol", [128, CH, M, B + 4], F32, g1)
    kb_ring = sb("kb_ring", [128, 2, M, N], F32, g1)
    cmp = sb("cmp", [128, 3, N], F16, g1)
    cnt = sb("cnt", [128, 3, M * CH], F32, g1)
    st = [sb(f"st{i}", [128, STEPS, 6], F32, g1) for i in range(2)]
    stx = sb("stx", [64, PAIRS, 6], F32, g1)
    mv = sb("mv", [128, PAIRS, 2], F32, g1)
    rs = sb("rs", [128, PAIRS, 2], F32, g1)
    mt_ = [sb(f"mt{i}", [128, 4], F32, g1) for i in range(2)]
    mh = [sb(f"mh{i}", [64, 10], F32, g1) for i in range(2)]
    P1H = sb("P1H", [128, 2, 2, CH, N], F16, g1)
    C2H = sb("C2H", [128, 2, TW], F16, g1)
    TT = sb("TT", [128, CH, 2, 2, C], F16, g1)
    R = sb("R", [128, 2, 2, 2, 2, POSW], F16, g1)
    LB = sb("LB", [128, 2, 2, 2, POSW, HG], F16, g1)
    Vr = sb("Vr", [128, 3, 2 * BLKS * 128], F32, g1)
    aM = sb("aM", [128, STEPT], F32, g1)
    MTs = sb("MTs", [120, 4 * 8], BF16, g1)
    MTe = sb("MTe", [120, 4 * 128], BF16, g1)
    raw = [sb(f"raw{i}", [128, TW], F32, g1) for i in range(2)]
    Wl = [sb(f"Wl{i}", [64, 256], F32, g1) for i in range(2)]
    Wc = [sb(f"Wc{i}", [64, OUTC[i]], F32, g1) for i in range(2)]
    bl = [sb(f"bl{i}", [64, 1], F32, g1) for i in range(2)]
    WD = [sb(f"WD{i}", [128, OUTC[i]], F32, g1) for i in range(2)]
    W4 = [sb(f"W4{i}", [128, OUTC[i]], F32, g1) for i in range(2)]
    WB = [sb(f"WB{i}", [128, HG, OUTC[i]], F32, g1) for i in range(2)]
    WBs = [sb(f"WBs{i}", [128, 3, HG * OUTC[i]], BF16, g1) for i in range(2)]
    Wcc = [sb(f"Wcc{i}", [128, 2 * OUTC[i]], F32, g1) for i in range(2)]
    Ws = [sb(f"Ws{i}", [128, 3, 2 * OUTC[i]], BF16, g1) for i in range(2)]
    be = [sb(f"be{i}", [128, 1], F32, g1) for i in range(2)]
    W3ab = sb("W3ab", [128, 64], F32, g1)
    W3c = sb("W3c", [128, 64], F32, g1)
    kc_b = sb("kc_b", [128, M, CH], F32, g1)
    early = ExitStack()
    coord = sb("coord", [48, N], F32, early)
    qf = sb("qf", [48, 3, N], F32, early)
    qi = sb("qi", [48, N], I32, early)
    cs = sb("cs", [48, 8], F32, early)
    XQ = sb("XQ", [128, 3, 64], I32, early)
    HX = sb("HX", [128, 3, 2, 64], I32, early)
    hm = sb("hm", [128, 4, 2, 64], I32, early)
    SP1 = sb("SP1", [128, 3, 3, 64], I32, early)
    KEY = sb("KEY", [128, M, 64], I32, early)
    KEYT = sb("KEYT", [128, M, 64], I32, early)
    K64 = sb("K64", [64, N], F32, early)
    XS = sb("XS", [128, 3, 3, 64], I32, early)
    early.close()
    late = ExitStack()
    VP = sb("VP", [128, len(VUNITS[1]), N], F32, late)
    S = sb("S", [128, 2, NCOL], F32, late)
    A = sb("A", [128, 2, NCOL], F32, late)
    AN = sb("AN", [128, 2, NCOL], F32, late)
    rZ = sb("rZ", [128, 2, NCOL], F32, late)
    lnZ = sb("lnZ", [128, 2, NCOL], F32, late)
    fy = sb("fy", [128, N], F32, late)
    F2 = sb("F2", [128, N], F32, late)
    xt = sb("xt", [64, N], F32, late)
    XC = sb("XC", [128, N], F32, late)
    late.close()
    g1.close()

    g2 = ExitStack()
    XN = sb("XN", [128, TILES, HID], F32, g2)
    LN = sb("LN", [128, TILES, HID], F32, g2)
    XT = sb("XT", [128, KC, TOKENS], F32, g2)
    wqkv = sb("wqkv", [128, 2, KC, (REP + 2) * DH], F32, g2)
    wo = sb("wo", [128, 2, REP, HID], F32, g2)
    bq = sb("bq", [128, NHEAD], F32, g2)
    bk = sb("bk", [128, NGRP], F32, g2)
    bv = sb("bv", [1, NGRP * DH], F32, g2)
    bo = sb("bo", [1, HID], F32, g2)
    ones_row = sb("ones_row", [1, 128], F32, g2)
    cosT = sb("cosT", [128, C], F32, g2)
    sinT = sb("sinT", [128, C], F32, g2)
    causal = sb("causal", [128, C], F32, g2)
    r1 = sb("r1", [128, 2, TOKENS], F32, g2)
    r2 = sb("r2", [128, 2, TOKENS], F32, g2)
    kT = sb("kT", [128, TOKENS], F32, g2)
    qT = sb("qT", [128, B, REP, C], F32, g2)
    vt = sb("vt", [128, TILES, DH], F32, g2)
    pr = sb("pr", [128, B, C], F32, g2)
    pm = sb("pm", [128, 3, B], F32, g2)
    PT = sb("PT", [128, TILES, 4, 128], F32, g2)
    CT = sb("CT", [128, TILES, REP, 4, C], F32, g2)
    st2 = sb("st2", [128, TILES, 6], F32, g2)
    mv2 = sb("mv2", [128, TILES, 2], F32, g2)
    rs2 = sb("rs2", [128, TILES, 2], F32, g2)
    fWq = sb("fWq", [128, KC, BOT], F32, g2)
    fWr = sb("fWr", [BOT, RDIM], F32, g2)
    akT = sb("akT", [BOT, NSLOT], F32, g2)
    avT = sb("avT", [128, KC, NSLOT], F32, g2)
    wvd = sb("wvd", [128, KC, VB], F32, g2)
    wvu = sb("wvu", [VB, HID], F32, g2)
    wu1 = sb("wu1", [128, KC, 128], F32, g2)
    bu1 = sb("bu1", [128, 1], F32, g2)
    wu2 = sb("wu2", [128, 1], F32, g2)
    lrel = sb("lrel", [128, NSLOT], F32, g2)
    sc3 = sb("sc3", [128, 3], F32, g2)
    ones_sq = sb("ones_sq", [128, 128], F32, g2)
    quT = sb("quT", [BOT, TOKENS], F32, g2)
    rqT = sb("rqT", [RDIM, TOKENS], F32, g2)
    rkT = sb("rkT", [RDIM, NSLOT], F32, g2)
    t1T = sb("t1T", [VB, NSLOT], F32, g2)
    AV = sb("AV", [NSLOT, HID], F32, g2)
    gl = sb("gl", [128, 4, TOKENS], F32, g2)
    rt = sb("rt", [128, TILES, NSLOT], F32, g2)
    rp = sb("rp", [128, TILES, NSLOT], F32, g2)
    at = sb("at", [128, TILES, NSLOT], F32, g2)
    wT = sb("wT", [128, TILES, 128], F32, g2)
    top = sb("top", [128, TILES, 8], F32, g2)
    gt = sb("gt", [128, 12, TILES], F32, g2)
    bg = sb("bg", [128, REP + 1], F32, g2)
    g2.close()

    consts_in = sem("consts_in")
    x_in = sem("x_in")
    coord_in = sem("coord_in")
    w_in = sem("w_in")
    vec = sem("vec_order")
    act_order = sem("act_order")
    pool_order = sem("pool_order")
    casts_done = sem("casts_done")
    zeros_done = sem("zeros_done")
    q_ready = sem("q_ready")
    q_out = sem("q_out")
    q_back = sem("q_back")
    key_ready = sem("key_ready")
    key_out = sem("key_out")
    key_back = sem("key_back")
    key_turned = sem("key_turned")
    kcol_ready = sem("kcol_ready")
    kb_in = [sem(f"kb_in{i}") for i in range(2)]
    kb_used = sem("kb_used")
    weff_mm = sem("weff_mm")
    weff_ev = sem("weff_ev")
    ln_var = sem("ln_var")
    ln_std = sem("ln_std")
    pair_done = sem("pair_done")
    fs_ready = sem("fs_ready")
    ctr_in = sem("ctr_in")
    ctr_out = sem("ctr_out")
    turned = sem("turned")
    tt_ready = sem("tt_ready")
    perm_mm = sem("perm_mm")
    perm_ev = sem("perm_ev")
    lb_ready = sem("lb_ready")
    ga_ready = sem("ga_ready")
    s_ready = sem("s_ready")
    mt_ready = sem("mt_ready")
    mts_ready = sem("mts_ready")
    mb_ready = sem("mb_ready")
    d_ready = sem("d_ready")
    e_ready = sem("e_ready")
    z_ready = sem("z_ready")
    rz_ready = sem("rz_ready")
    ln_ready = sem("ln_ready")
    an_ready = sem("an_ready")
    o_ready = sem("o_ready")
    o_used = sem("o_used")
    h3_mm = sem("h3_mm")
    graph_done = sem("graph_done")
    xn_in = sem("xn_in")
    aw_in = sem("aw_in")
    fw_in = sem("fw_in")
    wqkv_in = [sem(f"wqkv_in{i}") for i in range(2)]
    wo_in = [sem(f"wo_in{i}") for i in range(2)]
    wo_used = sem("wo_used")
    fill2 = sem("fill2")
    ln2_var = sem("ln2_var")
    ln2_std = sem("ln2_std")
    ln2_ready = sem("ln2_ready")
    xt_mm = sem("xt_mm")
    xt_ready = sem("xt_ready")
    proj_mm = sem("proj_mm")
    rope_parts = sem("rope_parts")
    qk_ready = sem("qk_ready")
    v_mm = sem("v_mm")
    vt_ready = sem("vt_ready")
    sc_mm = sem("sc_mm")
    sm_ready = sem("sm_ready")
    ex_ready = sem("ex_ready")
    pr_ready = sem("pr_ready")
    pt_mm = sem("pt_mm")
    pt_ready = sem("pt_ready")
    ctx_mm = sem("ctx_mm")
    ct_ready = sem("ct_ready")
    acc_mm = sem("acc_mm")
    ffn_mm = sem("ffn_mm")
    ffn_act = sem("ffn_act")
    ffn_vec = sem("ffn_vec")
    out_written = sem("out_written")
    w_split = sem("w_split")
    mte_ready = sem("mte_ready")
    vp_mm = sem("vp_mm")
    vp_ready = sem("vp_ready")
    v_out = sem("v_out")
    v_in = [sem(f"v_in{i}") for i in range(3)]
    xt_in = sem("xt_in")
    onehot_ready = sem("onehot_ready")
    pad_ready = sem("pad_ready")
    half_ready = sem("half_ready")
    lba_ready = sem("lba_ready")
    var_ready = sem("var_ready")
    std_ready = sem("std_ready")
    feat = sem("feat_order")
    f2_ready = sem("f2_ready")
    var3_ready = sem("var3_ready")
    std3_ready = sem("std3_ready")
    slots_zero = sem("slots_zero")
    kc_ready = sem("kc_ready")
    compared = sem("compared")
    COMPARES = M * (3 * CH - 1)
    rank_ready = sem("rank_ready")
    w4_ready = sem("w4_ready")
    am_ready = sem("am_ready")
    prep = sem("prep")
    soft = sem("soft")
    bg_ready = sem("bg_ready")
    row_ready = sem("row_ready")
    SOFT = 4
    FEAT = (3, 7)

    q_dram = nc.dram_tensor("q_scratch", [3, B * N], I32, kind="Internal").ap()
    v_dram = [nc.dram_tensor(f"values_scratch{L}", [2, 2, POSW, HG * OUTC[L]], F32, kind="Internal").ap()
              for L in range(2)]
    c_dram = nc.dram_tensor("centre_scratch", [2, 2, 2, C, N], F16, kind="Internal").ap()
    k_dram = nc.dram_tensor("key_scratch", [M, (B + 6) * N], I32, kind="Internal").ap()

    class Order:

        def __init__(self, eng, s):
            self.eng, self.s, self.n = eng, s, 0

        def did(self, ins):
            ins.then_inc(self.s, 1)
            self.n += 1
            return ins

        def sync(self):
            self.eng.wait_ge(self.s, self.n)

        def step(self, ins):
            self.did(ins)
            self.sync()

    TICKS = 2 * STEPS + 4

    def steps_of(L, i):
        n = i * 2 + L * PAIRS
        return [(u, n + u, n * STEPS + u * STEPS) for u in range(2)]

    def place(T, k):
        g = T - k
        return (g // STEPS, g % STEPS, g) if 0 <= g < 2 * STEPS else None

    def v_stored(L, n):
        one, first = [sum(len({b for b, _ in unit}) for unit in units) * 16 for units in (VUNITS[L], VUNITS[0])]
        return n * one if L == 0 else (n - PAIRS) * one + PAIRS * first

    block = ctx.enter_context(nc.Block())
    from_pairs = lambda a: a.rearrange("(q b) c n -> (b c) q n", b=2)

    @block.sync
    def _(sp):
        for d in range(3):
            sp.dma_start(coord[B * d:B * d + B, :], io["ctx_4096"][:, d, :]).then_inc(coord_in, 16)
        for name, tile in small.items():
            sp.dma_start(tile[:, :], io[name]).then_inc(consts_in, 16)
        sp.dma_start(FF[:, PAIRS:2 * PAIRS, :], from_pairs(io["x"])).then_inc(x_in, 16)
        for i in range(2):
            sp.dma_start(Wl[i][:, :], io[f"wlin{i}"]).then_inc(w_in, 16)
            sp.dma_start(Wc[i][:, :], io[f"wconv{i}T"]).then_inc(w_in, 16)
            sp.dma_start(bl[i][:, :], io[f"blin{i}"].rearrange("(k a) -> k a", a=1)).then_inc(w_in, 16)
        sp.wait_ge(zeros_done, 1)
        for b in range(2):
            r, c = slice(32 * b, 32 * b + 32), slice(32 * b, 32 * b + 32)
            sp.dma_start(W3ab[r, c], io["wconv3T"][0:32, :]).then_inc(w_in, 16)
            sp.dma_start(W3ab[64 + 32 * b:96 + 32 * b, c], io["wconv3T"][32:64, :]).then_inc(w_in, 16)
            sp.dma_start(W3c[64 * b:64 * b + 64, c], io["wconv3T"][64:128, :]).then_inc(w_in, 16)
        sp.wait_ge(q_ready, 1)
        for d in range(3):
            sp.dma_start(q_dram[d, :].rearrange("(b n) -> b n", n=N), qi[B * d:B * d + B, :]).then_inc(q_out, 16)
        sp.wait_ge(q_out, 48)
        sp.dma_start(XQ[:, :, :], q_dram.rearrange("d (p n) -> p d n", n=64)).then_inc(q_back, 16)
        sp.wait_ge(key_ready, 1)
        sp.dma_start(k_dram[:, 0:B * N].rearrange("m (p n) -> p m n", n=64), KEY[:, :, :]).then_inc(key_out, 16)
        sp.dma_start(k_dram[:, B * N:].rearrange("m (p n) -> p m n", n=64), KEY[0:6 * N // 64, :, :])\
          .then_inc(key_out, 16)
        sp.wait_ge(key_out, 32)
        for m in range(M):
            sp.dma_start(K64[B * m:B * m + B, :], k_dram[m, 0:B * N].rearrange("(b n) -> b n", n=N).bitcast(F32))\
              .then_inc(key_back, 16)

        def key_rows(pair, w):
            sp.dma_start(kb_ring[:, w, :, :],
                         k_dram[:, bass.ds(pair * 2 * N + w * N, N)].bitcast(F32).partition_broadcast(128))\
              .then_inc(kb_in[w], 16)

        for pair in range(3):
            for w in range(2):
                if pair:
                    sp.wait_ge(kb_used, 1 + 2 * pair + w - 1)
                key_rows(pair, w)

        def centres(n, u):
            sp.wait_ge(fs_ready, n + 1)
            for half in range(2):
                sp.dma_start(c_dram[u, :, half], C2H[64 * half:64 * half + 64, u, 0:N]).then_inc(ctr_out, 16)
            sp.wait_ge(ctr_out, n * 32 + 32)
            for m in range(M):
                sp.dma_start(R[32 * m:32 * m + 32, u, :, :, 1, 0:N].rearrange("c b h n -> c (b h) n"),
                             c_dram[u].rearrange("b h c n -> c (b h) n")).then_inc(ctr_in, 16)

        centres(0, 0)
        for L in range(2):
            oc = OUTC[L]
            wide = HG * oc
            nunit = len(VUNITS[L])
            if L == 1:
                sp.wait_ge(slots_zero, 2)
            with sp.Fori(0, PAIRS // 2) as i:
                for u, n, base in steps_of(L, i):
                    out0 = n * nunit if L == 0 else (n - PAIRS) * nunit + PAIRS * len(VUNITS[0])
                    for j, unit in enumerate(VUNITS[L]):
                        sp.wait_ge(vp_ready, out0 + (j + 1))
                        for b in sorted({b for b, _ in unit}):
                            cs_ = [c for bb, c in unit if bb == b]
                            p = VCH[cs_[0]]
                            col = [k for k, (bb, _) in enumerate(unit) if bb == b][0] * wide
                            dst = v_dram[L][u, b, 128 * cs_[0]:128 * cs_[0] + p * len(cs_), :]
                            sp.dma_start(dst.rearrange("(c p) n -> p c n", p=p),
                                         VP[0:p, j, col:col + wide * len(cs_)].rearrange("p (c n) -> p c n", n=wide))\
                              .then_inc(v_out, 16)
                    sp.wait_ge(v_out, v_stored(L, n + 1))
                    sp.nop(nofuse=True)
                    for c in range(CHUNKS):
                        if c == 4:
                            centres(n + 1, 1 - u)
                        nst = min(2, STEPS - 2 * c)
                        if c >= 3:
                            sp.wait_ge(o_ready, base + (2 * c - 4))
                        elif u == 1:
                            sp.wait_ge(o_ready, base + (2 * c - 3) if c < 2 else base)
                        for b in range(2):
                            vd = v_dram[L]
                            src = bass.AP(tensor=vd.tensor,
                                          offset=vd.offset + ((u * 2 + b) * POSW + 2 * c * STEPT) * wide,
                                          ap=[[oc, 64], [TOK * wide, nst * BLKS], [1, oc]])
                            dst = view(Vr, slice(64 * b, 64 * b + 64), (c % 3) * 2 * BLKS * 128 + b * oc,
                                       [[2 * oc, nst * BLKS], [1, oc]])
                            sp.dma_start(dst, src).then_inc(v_in[c % 3], 16)
                    if L == 0:
                        for w in range(2):
                            sp.wait_ge(kb_used, 1 + 2 * (n + 2) + (w + 1))
                            sp.nop(nofuse=True)
                            key_rows(n + 3, w)
                    if L == 1:
                        sp.wait_ge(pair_done, 1 + n)
                        sp.nop(nofuse=True)
                        q = i * 2 + u
                        sp.dma_start(xt[:, :], from_pairs(io["x"])[:, bass.ds(q, 1), :]).then_inc(xt_in, 16)
                        sp.dma_start(XC[0:64, :], FF[:, bass.ds(q, 1), :]).then_inc(xt_in, 16)
                        sp.dma_start(XC[64:128, :], FF[:, bass.ds(q + PAIRS, 1), :]).then_inc(xt_in, 16)
        sp.wait_ge(graph_done, 1)
        for u in range(2):
            sp.dma_start(XN[64 * u:64 * u + 64, :, :], FF[:, PAIRS:2 * PAIRS, :].rearrange("p (t u) n -> p u t n", u=2)[:, u, :, :])\
              .then_inc(xn_in, 16)
        for tile, name in ((cosT, "cos"), (sinT, "sin"), (causal, "causal")):
            sp.dma_start(tile[:, :], io[name]).then_inc(aw_in, 16)
        sp.dma_start(bq[:, :], io["bqT"]).then_inc(aw_in, 16)
        sp.dma_start(bk[:, :], io["bkT"]).then_inc(aw_in, 16)
        sp.dma_start(bv[:, :], io["bv"].rearrange("(a n) -> a n", a=1)).then_inc(aw_in, 16)
        sp.dma_start(bo[:, :], io["bo"].rearrange("(a n) -> a n", a=1)).then_inc(aw_in, 16)
        wq_v = io["Wq"].rearrange("(k p) n -> p k n", p=128)
        wk_v = io["Wk"].rearrange("(k p) n -> p k n", p=128)
        wv_v = io["Wv"].rearrange("(k p) n -> p k n", p=128)
        wo_v = io["Wo"].rearrange("(h p) n -> p h n", p=128)
        with sp.Fori(0, NGRP // 2) as h:
            for u in range(2):
                sp.wait_ge(v_mm, 1 + h * 2)
                sp.dma_start(wqkv[:, u, :, 0:REP * DH],
                             wq_v[:, :, bass.ds(h * (2 * REP * DH) + u * REP * DH, REP * DH)]).then_inc(wqkv_in[u], 16)
                sp.dma_start(wqkv[:, u, :, REP * DH:(REP + 1) * DH],
                             wk_v[:, :, bass.ds(h * (2 * DH) + u * DH, DH)]).then_inc(wqkv_in[u], 16)
                sp.dma_start(wqkv[:, u, :, (REP + 1) * DH:],
                             wv_v[:, :, bass.ds(h * (2 * DH) + u * DH, DH)]).then_inc(wqkv_in[u], 16)
                sp.wait_ge(wo_used, 1 + h * 2)
                sp.dma_start(wo[:, u, :, :], wo_v[:, bass.ds(h * (2 * REP) + u * REP, REP), :]).then_inc(wo_in[u], 16)
        kp = lambda a: a.rearrange("(k p) n -> p k n", p=128)
        for tile, src in ((fWq, kp(io["fWqT"])), (avT, kp(io["avT"])), (wvd, kp(io["WvdT"])), (wu1, kp(io["Wu1T"])),
                          (fWr, io["WrT"]), (akT, io["akT"]), (wvu, io["WvuT"]),
                          (bu1, io["bu1"].rearrange("(p a) -> p a", a=1)), (wu2, io["Wu2T"]),
                          (lrel, io["log_rel"].partition_broadcast(128))):
            sp.dma_start(tile[...], src).then_inc(fw_in, 16)
        for i, name in enumerate(("bu2", "gate_w1", "gate_bias")):
            sp.dma_start(sc3[:, i:i + 1], io[name].partition_broadcast(128)).then_inc(fw_in, 16)
        tokens = lambda a: a.rearrange("(t b) c n -> (b c) t n", b=4)
        for t in range(TILES):
            sp.wait_ge(row_ready, t + 1)
            sp.dma_start(tokens(out)[:, t, :], XN[:, t, :]).then_inc(out_written, 16)
        sp.wait_ge(out_written, 16 * TILES)

    @block.gpsimd
    def _(pool):
        o = Order(pool, pool_order)
        for t in (W3ab, W3c, Wcc[0], Wcc[1]):
            o.did(pool.memset(t[...], 0.0))
        o.did(pool.memset(FF[:, 2 * PAIRS, :], 0.0))
        for u in range(2):
            o.did(pool.memset(R[:, u, :, :, 1, :], 0.0))
        o.did(pool.memset(C2H[:, :, N:TW], 0.0))
        pool.memset(Vr[:, :, :], 0.0).then_inc(slots_zero, 1)
        o.did(pool.memset(eps_col[:, :], EPS))
        for i, s in enumerate((pair_done, kb_used, v_mm, wo_used, sc_mm, ctx_mm, qk_ready, ct_ready, pt_ready)):
            pool.memset(started[:, i:i + 1], 0.0).then_inc(s, 1)
        o.sync()
        pool.wait_ge(consts_in, 16 * len(small))
        o.did(pool.tensor_copy(ident_bf[:, :], ident[:, :]))
        o.did(pool.tensor_copy(ident_h[:, :], ident[:, :]))
        o.sync()
        pool.memset(cnt[:, :, :], 0.0).then_inc(zeros_done, 1)
        def sorted_by_head(n, u, b):
            pool.wait_ge(pad_ready, n * 2 + (b + 1))
            pool.nop(nofuse=True)
            for h in range(2):
                ins = pool.tensor_scalar(LB[:, u, b, :, :, h], R[:, u, b, :, 0, :], headmask[:, h:h + 1], 1.0,
                                         ALU.mult, ALU.mult)
            ins.then_inc(half_ready, 1)

        for b in range(2):
            pool.wait_ge(pad_ready, b + 1)
            sorted_by_head(0, 0, b)
        for L in range(2):
            if L == 1:
                pool.wait_ge(pair_done, 1 + PAIRS)
                pool.memset(Vr[:, :, :], 0.0).then_inc(slots_zero, 1)
            with pool.Fori(0, PAIRS // 2) as i:
                pairs = steps_of(L, i)
                base0 = pairs[0][2]
                for T in range(TICKS):
                    if place(T, 2):
                        u, t, g = place(T, 2)
                        pool.wait_ge(rz_ready, base0 + (g + 1))
                        if g >= 2:
                            pool.wait_ge(o_ready, base0 + (g - 1))
                        pool.tensor_tensor(AN[:, g % 2, :], A[:, g % 2, :], rZ[:, g % 2, :], ALU.mult)\
                            .then_inc(an_ready, 1)
                    if place(T, 0):
                        u, t, g = place(T, 0)
                        if t in (7, 9):
                            sorted_by_head(pairs[u][1] + 1, 1 - u, (t - 7) // 2)
        pool.wait_ge(graph_done, 1)
        pool.memset(PT[...], 0.0).then_inc(fill2, 1)
        pool.memset(ones_row[:, :], 1.0).then_inc(fill2, 1)
        pool.memset(ones_sq[:, :], 1.0).then_inc(fill2, 1)
        with pool.Fori(0, NGRP) as g:
            for j in range(REP + 1):
                pool.wait_ge(rope_parts, g * (REP + 1) + j + 1)
                if j == 0:
                    pool.wait_ge(sc_mm, 1 + g)
                dst = kT[:, :] if j == 0 else qT[:, :, j - 1, :]
                by_b = (lambda a: a) if j == 0 else (lambda a: a.rearrange("p (b s) -> p b s", b=B))
                pool.tensor_tensor(dst, by_b(r1[:, j % 2, :]), by_b(r2[:, j % 2, :]), ALU.add).then_inc(qk_ready, 1)

    @block.scalar
    def _(act):
        for L in range(2):
            oc = OUTC[L]
            act.wait_ge(weff_mm, 3 * L + 1)
            act.activation(WD[L][:, :], ps_ga[:, 0:oc], ACT.Copy).then_inc(weff_ev, 1)
            act.wait_ge(weff_mm, 3 * L + 2)
            act.wait_ge(zeros_done, 1)
            for r in range(4):
                q = (r % 2) * oc
                act.activation(Wcc[L][32 * r:32 * r + 32, q:q + oc], ps_p[32 * r:32 * r + 32, 0:oc], ACT.Copy)\
                   .then_inc(act_order, 1)
            act.wait_ge(weff_mm, 3 * L + 3)
            act.activation(be[L][0:2 * oc, :], ps_mb[0:2 * oc, 0:1], ACT.Copy).then_inc(weff_ev, 1)
        act.wait_ge(key_turned, 1)
        turned_keys = ps_mt[:, 0:CH * 64].rearrange("p (c m b) -> p c m b", c=CH, m=M)
        act.activation(kcol[:, :, :, 0:B], turned_keys, ACT.Copy)
        act.activation(kcol[:, :, :, B:B + 4], turned_keys[:, :, :, 0:4], ACT.Copy).then_inc(kcol_ready, 1)
        act.wait_ge(ln_var, 1)
        act.activation(rs[0:64, :, 0], mv[0:64, :, 1], ACT.Sqrt, bias=eps_col[0:64, :]).then_inc(ln_std, 1)

        def turned_points(n):
            act.wait_ge(turned, n + 1)
            for half in range(2):
                ins = act.activation(TT[:, :, :, half, :],
                                     ps_t[:, 0:CH * 128].rearrange("p (k h b c) -> p k h b c", h=2, b=2, c=C)[:, :, half],
                                     ACT.Copy)
            ins.then_inc(tt_ready, 1)

        def sorted_points(n, u, k):
            b, mp = k // 2, k % 2
            act.wait_ge(perm_mm, n * 4 + (k + 1))
            for m in range(2):
                for half in range(2):
                    r0 = 64 * m + 32 * half
                    d0 = 32 * (2 * mp + m)
                    ins = act.activation(R[d0:d0 + 32, u, b, half, 0, PADL:PADL + N],
                                         (ps_p[:, :], ps_t32)[k % 2][r0:r0 + 32, :], ACT.Copy)
            ins.then_inc(perm_ev, 1)

        def sorted_by_head(n, u, b):
            act.wait_ge(pad_ready, n * 2 + (b + 1))
            for h in (2, 3):
                ins = act.activation(LB[:, u, b, :, :, h], R[:, u, b, :, 0, :], ACT.Copy, scale=headmask[:, h:h + 1])
            ins.then_inc(lba_ready, 1)

        def value_units(L, n, u, t):
            nunit = len(VUNITS[L])
            out0 = n * nunit if L == 0 else (n - PAIRS) * nunit + PAIRS * len(VUNITS[0])
            for j, unit in enumerate(VUNITS[L]):
                if (j >= VFIRST[L]) != t:
                    continue
                act.wait_ge(vp_mm, out0 + (j + 1))
                if j == 0 and u == 1:
                    act.wait_ge(v_out, v_stored(L, n))
                p = VCH[unit[0][1]]
                w = len(unit) * HG * OUTC[L]
                act.activation(VP[0:p, j, 0:w], (ps_p[:, :], ps_t32)[j % 2][0:p, 0:w], ACT.Copy)\
                   .then_inc(vp_ready, 1)

        def load_exp_ln():
            act.nop(nofuse=True)
            act.add_instruction(mybir.InstLoadActFuncSet(act_func_set_id=EXP_LN_SET, name=nc.get_next_instruction_name(),
                                                         engine=mybir.EngineType.Activation))

        turned_points(0)
        for k in range(4):
            sorted_points(0, 0, k)
        for b in range(2):
            sorted_by_head(0, 0, b)
        for L in range(2):
            with act.Fori(0, PAIRS // 2) as i:
                pairs = steps_of(L, i)
                base0 = pairs[0][2]
                act.wait_ge(pair_done, 1 + pairs[0][1])
                load_exp_ln()

                def std(u, n):
                    act.wait_ge(var_ready, n + 1)
                    act.activation(mt_[u][0:2 * OUTC[L], 3:4], mt_[u][0:2 * OUTC[L], 1:2], ACT.Sqrt,
                                   bias=eps_col[0:2 * OUTC[L], :]).then_inc(std_ready, 1)

                def std3(u, n):
                    act.wait_ge(var3_ready, n - (PAIRS - 1))
                    act.activation(mh[u][:, 2:3], mh[u][:, 1:2], ACT.Sqrt, bias=eps_col[0:64, :])\
                       .then_inc(std3_ready, 1)

                for T in range(TICKS):
                    if T == STEPS + 4:
                        std(0, pairs[0][1])
                        load_exp_ln()
                    if L == 1 and T == STEPS + 10:
                        std3(0, pairs[0][1])
                        load_exp_ln()
                    if place(T, 1):
                        u, t, g = place(T, 1)
                        act.wait_ge(d_ready, base0 + (g + 1))
                        if g >= 2:
                            act.wait_ge(an_ready, base0 + (g - 1))
                        act.activation(A[:, g % 2, :], S[:, g % 2, :], ACT.Exp, scale=1.0 / math.sqrt(HD))\
                           .then_inc(e_ready, 1)
                    if place(T, 2):
                        u, t, g = place(T, 2)
                        act.wait_ge(z_ready, base0 + (g + 1))
                        act.activation(lnZ[:, g % 2, :], ps_z[:, 0:NCOL], ACT.Ln).then_inc(ln_ready, 1)
                        act.wait_ge(ln_ready, base0 + (g + 1))
                        if g >= 2:
                            act.wait_ge(an_ready, base0 + (g - 1))
                        act.activation(rZ[:, g % 2, :], lnZ[:, g % 2, :], ACT.Exp, scale=-1.0).then_inc(rz_ready, 1)
                    if place(T, 0):
                        u, t, g = place(T, 0)
                        act.wait_ge(mts_ready, base0 + (g + 1))
                        if g >= 1:
                            act.wait_ge(mb_ready, base0 + g)
                        act.activation(view(MTe, slice(0, 120), 0, [[HG * WIN, 8], [HG, WIN], [1, HG]]),
                                       view(MTs, slice(0, 120), 0, [[HG, 8], [0, WIN], [1, HG]]), ACT.Copy)\
                           .then_inc(mte_ready, 1)
                        n1 = pairs[u][1] + 1
                        if t < 2:
                            value_units(L, pairs[u][1], u, t)
                        if t == 4:
                            turned_points(n1)
                        if 5 <= t < 9:
                            sorted_points(n1, 1 - u, t - 5)
                        if t in (7, 9):
                            sorted_by_head(n1, 1 - u, (t - 7) // 2)
                std(1, pairs[1][1])
                if L == 1:
                    std3(1, pairs[1][1])
        act.wait_ge(ln2_var, 1)
        act.activation(rs2[:, :, 0], mv2[:, :, 1], ACT.Sqrt, bias=eps_col[:, :]).then_inc(ln2_std, 1)
        for k in range(KC):
            act.wait_ge(xt_mm, k + 1)
            act.activation(XT[:, k, :], ps[k][:, :], ACT.Copy).then_inc(xt_ready, 1)
        with act.Fori(0, NGRP) as g:
            act.wait_ge(v_mm, 1 + g + 1)
            act.wait_ge(ctx_mm, 1 + g * TILES)
            act.activation(vt[:, :, :], ps[6][:, :].rearrange("p (t d) -> p t d", t=TILES), ACT.Copy)\
               .then_inc(vt_ready, 1)
            act.wait_ge(sm_ready, g + 1)
            act.activation(pr[:, :, :], pr[:, :, :], ACT.Exp).then_inc(ex_ready, 1)
            act.wait_ge(pt_mm, g + 1)
            for b in range(4):
                r = slice(32 * b, 32 * b + 32)
                ins = act.activation(PT[r, :, b, :], ps[6][r, :].rearrange("p (t k) -> p t k", t=TILES), ACT.Copy)
            ins.then_inc(pt_ready, 1)
            for t in range(TILES):
                act.wait_ge(ctx_mm, 1 + g * TILES + (t + 1))
                if t == 0:
                    act.wait_ge(wo_used, 1 + g)
                act.activation(CT[:, t, :, :, :].rearrange("p r b s -> p b r s"), ps[4 + t % 2][:, :].rearrange("p (b r s) -> p b r s", b=4, r=REP),
                               ACT.Copy).then_inc(ct_ready, 1)
        act.wait_ge(ln2_var, 2)
        act.activation(rs2[:, :, 0], mv2[:, :, 1], ACT.Sqrt, bias=eps_col[:, :]).then_inc(ln2_std, 1)
        for k in range(KC):
            act.wait_ge(xt_mm, KC + k + 1)
            act.activation(XT[:, k, :], ps[k][:, :], ACT.Copy).then_inc(xt_ready, 1)
        act.wait_ge(ffn_mm, 1)
        act.activation(quT[:, :], ps[4][0:BOT, :], ACT.Copy).then_inc(ffn_act, 1)
        act.wait_ge(ffn_mm, 2)
        act.activation(rkT[:, :], ps[5][0:RDIM, 0:NSLOT], ACT.Copy).then_inc(ffn_act, 1)
        act.wait_ge(ffn_mm, 3)
        act.activation(t1T[:, :], ps[6][0:VB, 0:NSLOT], ACT.Copy).then_inc(ffn_act, 1)
        act.wait_ge(ffn_mm, 4)
        act.activation(gl[:, 0, :], ps[0][:, :], ACT.Identity, bias=bu1[:, :]).then_inc(ffn_act, 1)
        act.wait_ge(ffn_mm, 5)
        act.activation(rqT[:, :], ps[1][0:RDIM, :], ACT.Copy).then_inc(ffn_act, 1)
        act.wait_ge(ffn_mm, 6)
        act.activation(AV[:, :], ps[2][:, :], ACT.Copy).then_inc(ffn_act, 1)
        act.wait_ge(ffn_vec, 1)
        act.activation(gl[:, 2, :], gl[:, 1, :], ACT.Tanh, scale=math.sqrt(2 / math.pi)).then_inc(ffn_act, 1)
        act.wait_ge(ffn_vec, 2)
        act.activation(gt[:, 0, :], mv2[:, :, 1], ACT.Ln, bias=1.0).then_inc(ffn_act, 1)
        act.wait_ge(ffn_vec, 4)
        act.activation(at[:, :, :], at[:, :, :], ACT.Exp).then_inc(ffn_act, 1)
        act.wait_ge(ffn_vec, 5)
        act.activation(gt[:, 4, :], gt[:, 3, :], ACT.Sigmoid).then_inc(ffn_act, 1)
        act.wait_ge(ffn_vec, 7)
        act.activation(gt[:, 8, :], gt[:, 7, :], ACT.Sigmoid).then_inc(ffn_act, 1)
        act.wait_ge(ffn_mm, 10)
        act.activation(wT[:, :, :], ps[5][:, :].rearrange("p (t k) -> p t k", t=TILES), ACT.Copy)\
           .then_inc(ffn_act, 1)

    ps_sc = ps_t[:, :].bitcast(F32)

    def attention_pe(pe):
        pe.wait_ge(fill2, 3)
        pe.wait_ge(aw_in, 16 * 7)

        def turn():
            for k in range(KC):
                for t in range(TILES):
                    ins = pe.transpose(ps[k][:, 128 * t:128 * t + 128], LN[:, t, 128 * k:128 * k + 128], ident[:, :])
                ins.then_inc(xt_mm, 1)

        pe.wait_ge(ln2_ready, 1)
        turn()
        pe.wait_ge(xt_ready, KC)
        for t in range(TILES):
            pe.matmul(ps[t][:, :], ones_row[:, :], bo[:, :], start=True, stop=False, skip_group_check=True)

        with pe.Fori(0, NGRP // 2) as h:
            for u in range(2):
                pe.wait_ge(wqkv_in[u], h * 48 + 48)
                heads = h * (2 * (REP + 1)) + u * (REP + 1)
                for j in range(REP + 1):
                    col = REP * DH if j == 0 else (j - 1) * DH
                    bank = ps[4 + j % 2]
                    if j >= 2:
                        pe.wait_ge(rope_parts, heads + (j - 1))
                    elif j == 0:
                        pe.wait_ge(ct_ready, 1 + h * (2 * TILES) + u * TILES)
                    for k in range(KC):
                        ins = pe.matmul(bank[:, :], wqkv[:, u, k, col:col + DH], XT[:, k, :],
                                        start=(k == 0), stop=(k == KC - 1))
                    ins.then_inc(proj_mm, 1)
                pe.wait_ge(pt_ready, 1 + h * 2 + u)
                col = (REP + 1) * DH
                for t in range(TILES):
                    for k in range(KC):
                        pe.matmul(ps[6][:, 128 * t:128 * t + 128], XT[:, k, 128 * t:128 * t + 128],
                                  wqkv[:, u, k, col:col + DH], start=(k == 0), stop=False)
                    ins = pe.matmul(ps[6][:, 128 * t:128 * t + 128], ones_row[:, :],
                                    bv[:, bass.ds(h * (2 * DH) + u * DH, DH)], start=False, stop=True)
                ins.then_inc(v_mm, 1)
                pe.wait_ge(qk_ready, 1 + heads + (REP + 1))
                pe.wait_ge(vt_ready, h * 2 + (u + 1))
                for b in range(B):
                    ins = pe.matmul(ps_sc[:, 32 * b:32 * b + 32], qT[:, b, :, :],
                                    kT[:, 32 * b:32 * b + 32], start=True, stop=True)
                ins.then_inc(sc_mm, 1)
                pe.wait_ge(pr_ready, h * 2 + (u + 1))
                for t in range(TILES):
                    ins = pe.transpose(ps[6][:, 128 * t:128 * t + 128], pr[:, 4 * t:4 * t + 4, :], ident[:, :])
                ins.then_inc(pt_mm, 1)
                pe.wait_ge(pt_ready, 1 + h * 2 + (u + 1))
                for t in range(TILES):
                    if t >= 2:
                        pe.wait_ge(ct_ready, 1 + h * (2 * TILES) + (u * TILES + t - 1))
                    pe.matmul(ps[4 + t % 2][:, :], vt[:, t, :], PT[:, t, :, :], start=True, stop=True)\
                      .then_inc(ctx_mm, 1)
                pe.wait_ge(wo_in[u], h * 16 + 16)
                for t in range(TILES):
                    pe.wait_ge(ct_ready, 1 + h * (2 * TILES) + (u * TILES + t + 1))
                    for r in range(REP):
                        ins = pe.matmul(ps[t][:, :], CT[:, t, r, :, :], wo[:, u, r, :], start=False, stop=False,
                                        skip_group_check=True)
                ins.then_inc(wo_used, 1)
        pe.wait_ge(fw_in, 16 * 13)
        pe.wait_ge(ln2_ready, 2)
        turn()
        pe.wait_ge(xt_ready, 2 * KC)
        for k in range(KC):
            ins = pe.matmul(ps[4][0:BOT, :], fWq[:, k, :], XT[:, k, :], start=(k == 0), stop=(k == KC - 1))
        ins.then_inc(ffn_mm, 1)
        pe.matmul(ps[5][0:RDIM, 0:NSLOT], fWr[:, :], akT[:, :], start=True, stop=True).then_inc(ffn_mm, 1)
        for k in range(KC):
            ins = pe.matmul(ps[6][0:VB, 0:NSLOT], wvd[:, k, :], avT[:, k, :], start=(k == 0), stop=(k == KC - 1))
        ins.then_inc(ffn_mm, 1)
        for k in range(KC):
            ins = pe.matmul(ps[0][:, :], wu1[:, k, :], XT[:, k, :], start=(k == 0), stop=(k == KC - 1))
        ins.then_inc(ffn_mm, 1)
        pe.wait_ge(ffn_act, 1)
        pe.matmul(ps[1][0:RDIM, :], fWr[:, :], quT[:, :], start=True, stop=True).then_inc(ffn_mm, 1)
        pe.wait_ge(ffn_act, 3)
        pe.matmul(ps[2][:, :], t1T[:, :], wvu[:, :], start=True, stop=True).then_inc(ffn_mm, 1)
        pe.wait_ge(ffn_act, 5)
        for t in range(TILES):
            ins = pe.matmul(ps[3][:, 128 * t:128 * t + 128], rqT[:, 128 * t:128 * t + 128], rkT[:, :],
                            start=True, stop=True)
        ins.then_inc(ffn_mm, 1)
        for t in range(TILES):
            ins = pe.matmul(ps[4][:, 128 * t:128 * t + 128], quT[:, 128 * t:128 * t + 128], akT[:, :],
                            start=True, stop=True)
        ins.then_inc(ffn_mm, 1)
        pe.wait_ge(ffn_vec, 3)
        pe.wait_ge(ffn_act, 8)
        pe.matmul(ps[6][:, 0:TILES], ones_sq[:, :], gt[:, 0, :], start=True, stop=True)
        for t in range(TILES):
            ins = pe.matmul(ps[6][:, 8 + t:9 + t], gl[:, 3, 128 * t:128 * t + 128], wu2[:, :], start=True, stop=True)
        ins.then_inc(ffn_mm, 1)
        pe.wait_ge(ffn_vec, 8)
        for t in range(TILES):
            ins = pe.transpose(ps[5][:, 128 * t:128 * t + 128], at[:, t, :], ident[:, :])
        ins.then_inc(ffn_mm, 1)
        pe.wait_ge(ffn_act, 12)
        for t in range(TILES):
            pe.matmul(ps[t][:, :], wT[:, t, :], AV[:, :], start=True, stop=True).then_inc(ffn_mm, 1)

    @block.tensor
    def _(pe):
        pe.wait_ge(w_in, 16 * 12)
        pe.wait_ge(consts_in, 16 * len(small))
        for L in range(2):
            oc = OUTC[L]
            if L:
                pe.wait_ge(weff_ev, 2)
            for part, off in ((0, 128), (1, 0)):
                for m in range(M):
                    mi = PERMS[L].index(m)
                    ins = pe.matmul(ps_ga[32 * m:32 * m + 32, part * 64:part * 64 + oc],
                                    Wl[L][:, off + mi:off + mi + 125:4], Wc[L][:, :], start=True, stop=True)
            ins.then_inc(weff_mm, 1)
            pe.wait_ge(w4_ready, L + 1)
            pe.matmul(ps_p[:, 0:oc], fold[:, :], W4[L][:, :], start=True, stop=True).then_inc(weff_mm, 1)
            for b in range(2):
                ins = pe.matmul(ps_mb[oc * b:oc * b + oc, 0:1], Wc[L][:, :], bl[L][:, :], start=True, stop=True)
            ins.then_inc(weff_mm, 1)
        pe.wait_ge(key_back, 64)
        for c in range(CH):
            ins = pe.transpose(ps_mt[:, 64 * c:64 * c + 64], K64[:, 128 * c:128 * c + 128], ident[0:64, 0:64])
        ins.then_inc(key_turned, 1)

        def turn_points(n, u):
            pe.wait_ge(fs_ready, n + 1)
            pe.nop(nofuse=True)
            for c in range(CH):
                ins = pe.transpose(ps_t[:, 128 * c:128 * c + 128], C2H[:, u, 128 * c:128 * c + 128], ident_h[:, :])
            ins.then_inc(turned, 1)

        def sort_points(n, k):
            b = k // 2
            pe.wait_ge(onehot_ready, n * 4 + (k + 1))
            if k == 0:
                pe.wait_ge(tt_ready, n + 1)
            elif k >= 2:
                pe.wait_ge(perm_ev, n * 4 + (k - 1))
            bank = (ps_p[:, :], ps_t32)[k % 2]
            for m in range(2):
                for c in range(CH):
                    ins = pe.matmul(bank[64 * m:64 * m + 64, :], TT[:, c, b, :, :], P1H[:, k % 2, m, c, :],
                                    start=(c == 0), stop=(c == CH - 1))
            ins.then_inc(perm_mm, 1)

        def values(L, n, u, t):
            wide = HG * OUTC[L]
            nunit = len(VUNITS[L])
            out0 = n * nunit if L == 0 else (n - PAIRS) * nunit + PAIRS * len(VUNITS[0])
            for j, unit in enumerate(VUNITS[L]):
                if (j >= VFIRST[L]) != t:
                    continue
                if j >= 2:
                    pe.wait_ge(vp_ready, out0 + (j - 1))
                bank = (ps_p[:, :], ps_t32)[j % 2]
                for k, (b, c) in enumerate(unit):
                    terms = ((0, 0), (0, 1), (0, 2), (1, 0), (1, 1))
                    for x, (half, part) in enumerate(terms):
                        ins = pe.matmul(bank[0:VCH[c], k * wide:k * wide + wide],
                                        R[:, u, b, half, 0, 128 * c:128 * c + VCH[c]], WBs[L][:, part, :],
                                        start=(x == 0), stop=(x == len(terms) - 1))
                ins.then_inc(vp_mm, 1)

        def scores(base0, u, t, g):
            if g >= 2:
                pe.wait_ge(s_ready, base0 + (g - 1))
            for k in range(BLKS):
                at0 = (t * BLKS + k) * TOK
                for b in range(2):
                    dst = ps_ga[64 * b:64 * b + 64, (g % 2) * 256 + 32 * k:(g % 2) * 256 + 32 * k + 32]
                    for j, (l, r) in enumerate(((0, 0), (0, 1), (1, 0))):
                        ins = pe.matmul(dst, LB[:, u, b, l, at0:at0 + WIN, :], R[:, u, b, r, :, at0:at0 + WIN],
                                        start=(j == 0), stop=(j == 2))
            ins.then_inc(ga_ready, 1)

        pe.wait_ge(zeros_done, 1)
        pe.wait_ge(w_split, 1)
        pe.wait_ge(kcol_ready, 1)
        turn_points(0, 0)
        for k in range(4):
            sort_points(0, k)
        for L in range(2):
            oc = OUTC[L]
            with pe.Fori(0, PAIRS // 2) as i:
                pairs = steps_of(L, i)
                base0 = pairs[0][2]
                pe.wait_ge(pair_done, 1 + pairs[0][1])

                def last_conv(u, n):
                    pe.wait_ge(f2_ready, n - (PAIRS - 1))
                    pe.wait_ge(perm_ev, pairs[1][1] * 4 + 8)
                    pe.nop(nofuse=True)
                    pe.wait_ge(xt_in, (n - PAIRS) * 48 + 48)
                    pe.nop(nofuse=True)
                    pe.matmul(ps_t32[0:64, :], W3ab[:, :], XC[:, :], start=True, stop=False)
                    pe.matmul(ps_t32[0:64, :], W3c[:, :], F2[:, :], start=False, stop=True).then_inc(h3_mm, 1)

                for T in range(TICKS):
                    if place(T, 0) and place(T, 0)[1] == 0:
                        u = place(T, 0)[0]
                        n = pairs[u][1]
                        pe.wait_ge(half_ready, n * 2 + 2)
                        pe.wait_ge(lba_ready, n * 2 + 2)
                        pe.wait_ge(ctr_in, n * 64 + 64)
                        if T == 0:
                            scores(base0, 0, 0, 0)
                    if place(T, 1):
                        u, t, g = place(T, 1)
                        pe.wait_ge(mte_ready, base0 + (g + 1))
                        if g >= 1:
                            pe.wait_ge(d_ready, base0 + g)
                        for j in range(4):
                            ins = pe.matmul(ps_mb[:, 120 * j:120 * j + 120], MTe[:, 128 * j:128 * j + 128],
                                            ident_bf[0:120, 0:120], start=True, stop=True)
                        ins.then_inc(mb_ready, 1)
                    if place(T, 2):
                        u, t, g = place(T, 2)
                        pe.wait_ge(e_ready, base0 + (g + 1))
                        if g >= 1:
                            pe.wait_ge(ln_ready, base0 + g)
                        pe.matmul(ps_z[:, 0:NCOL], group[:, :], A[:, g % 2, :], start=True, stop=True)\
                          .then_inc(z_ready, 1)
                    if place(T, 0):
                        u, t, g = place(T, 0)
                        pe.wait_ge(s_ready, base0 + (g + 1))
                        if g >= 1:
                            pe.wait_ge(mts_ready, base0 + g)
                        sbf = S[:, g % 2, :].bitcast(BF16)
                        for j in range(4):
                            ins = pe.matmul(ps_mt[0:120, 128 * j:128 * j + 128],
                                            sbf[:, 240 * j + 1:240 * j + 240:2], ident_bf[:, :],
                                            start=True, stop=True)
                        ins.then_inc(mt_ready, 1)
                        if place(T + 1, 0):
                            u1, t1, g1_ = place(T + 1, 0)
                            if t1 == 0:
                                n = pairs[u1][1]
                                pe.wait_ge(half_ready, n * 2 + 2)
                                pe.wait_ge(lba_ready, n * 2 + 2)
                                pe.wait_ge(ctr_in, n * 64 + 64)
                            scores(base0, u1, t1, g1_)
                    if place(T, 3):
                        u, t, g = place(T, 3)
                        dst = ps_o[g % 2]
                        if g >= 2:
                            pe.wait_ge(o_used, base0 + (g - 1))
                        for part in range(3):
                            pe.matmul(dst[0:2 * oc, 0:NCOL], Ws[L][:, part, :],
                                      view(C2H, slice(0, 128), u * TW + t * STEPT, [[1, STEPT], [0, K]]),
                                      start=(part == 0), stop=False, skip_group_check=True)
                        pe.wait_ge(an_ready, base0 + (g + 1))
                        c = t // 2
                        if t % 2 == 0:
                            pe.wait_ge(v_in[c % 3], pairs[u][1] * 64 + (32 * (c // 3) + 32))
                        for k in range(BLKS):
                            v0 = (t % 2 * BLKS + k) * 2 * oc
                            ins = pe.matmul(dst[0:2 * oc, 60 * k:60 * k + 60], Vr[:, c % 3, v0:v0 + 2 * oc],
                                            AN[:, g % 2, 60 * k:60 * k + 60], start=False, stop=(k == BLKS - 1),
                                            skip_group_check=True)
                        ins.then_inc(o_ready, 1)
                    if L == 1 and T == STEPS + 9:
                        last_conv(0, pairs[0][1])
                    if place(T, 0):
                        u, t, g = place(T, 0)
                        n1 = pairs[u][1] + 1
                        if t < 2:
                            values(L, pairs[u][1], u, t)
                        if t == 4:
                            turn_points(n1, 1 - u)
                        if 4 <= t < 8:
                            sort_points(n1, t - 4)
                if L == 1:
                    last_conv(1, pairs[1][1])
        attention_pe(pe)


    @block.vector
    def _(v):
        o = Order(v, vec)
        v.wait_ge(coord_in, 48)
        o.did(v.tensor_reduce(cs[:, 0:1], coord[:, :], AX, ALU.max))
        o.did(v.tensor_reduce(cs[:, 1:2], coord[:, :], AX, ALU.min))
        o.sync()
        o.step(v.tensor_tensor(cs[:, 2:3], cs[:, 0:1], cs[:, 1:2], ALU.subtract))
        o.step(v.tensor_scalar(cs[:, 3:4], cs[:, 2:3], 1e-6, None, ALU.add))
        o.step(v.reciprocal(cs[:, 4:5], cs[:, 3:4]))
        o.step(v.tensor_scalar(cs[:, 5:6], cs[:, 4:5], float(2 ** BITS - 1), None, ALU.mult))
        o.step(v.tensor_scalar(qf[:, 0, :], coord[:, :], cs[:, 1:2], cs[:, 5:6], ALU.subtract, ALU.mult))
        o.step(v.tensor_copy(qi[:, :], qf[:, 0, :]))
        o.step(v.tensor_copy(qf[:, 1, :], qi[:, :]))
        o.step(v.tensor_tensor(qf[:, 2, :], qf[:, 1, :], qf[:, 0, :], ALU.is_gt))
        o.step(v.tensor_tensor(qf[:, 1, :], qf[:, 1, :], qf[:, 2, :], ALU.subtract))
        o.step(v.tensor_scalar(qf[:, 1, :], qf[:, 1, :], 0.0, float(2 ** BITS - 1), ALU.max, ALU.min))
        v.tensor_copy(qi[:, :], qf[:, 1, :]).then_inc(q_ready, 1)
        v.wait_ge(q_back, 16)

        def interleave(x):
            for s, mask in ((16, 0x030000FF), (8, 0x0300F00F), (4, 0x030C30C3), (2, 0x09249249)):
                o.step(v.tensor_scalar(SP1[:, :, :, :], x, s, None, ALU.logical_shift_left))
                o.step(v.tensor_tensor(x, x, SP1[:, :, :, :], ALU.bitwise_or))
                o.step(v.tensor_scalar(x, x, mask, None, ALU.bitwise_and))

        for j in range(3):
            for w, src in enumerate((j, (1, 0, 2)[j])):
                o.did(v.tensor_copy(HX[:, j, w, :], XQ[:, src, :]))
        o.sync()
        h = [HX[:, j, :, :] for j in range(3)]
        msk, dif, tmp, acc = [hm[:, j, :, :] for j in range(4)]

        def bit_mask(dst, src, bit):
            o.step(v.tensor_scalar(dst, src, 31 - bit, None, ALU.logical_shift_left))
            o.step(v.tensor_scalar(dst, dst, 31, None, ALU.arith_shift_right))

        for bit in range(BITS - 1, 0, -1):
            low = (1 << bit) - 1
            bit_mask(msk, h[0], bit)
            o.step(v.tensor_scalar(msk, msk, low, None, ALU.bitwise_and))
            o.step(v.tensor_tensor(h[0], h[0], msk, ALU.bitwise_xor))
            for j in (1, 2):
                bit_mask(msk, h[j], bit)
                o.step(v.tensor_tensor(dif, h[0], h[j], ALU.bitwise_xor))
                o.step(v.tensor_tensor(dif, dif, msk, ALU.bitwise_or))
                o.step(v.tensor_scalar(tmp, dif, low, None, ALU.bitwise_and))
                o.step(v.tensor_tensor(h[0], h[0], tmp, ALU.bitwise_xor))
                o.step(v.tensor_tensor(dif, dif, msk, ALU.bitwise_xor))
                o.step(v.tensor_scalar(tmp, dif, low, None, ALU.bitwise_and))
                o.step(v.tensor_tensor(h[j], h[j], tmp, ALU.bitwise_xor))
        o.step(v.tensor_tensor(h[1], h[1], h[0], ALU.bitwise_xor))
        o.step(v.tensor_tensor(h[2], h[2], h[1], ALU.bitwise_xor))
        for n, bit in enumerate(range(BITS - 1, 0, -1)):
            low = (1 << bit) - 1
            bit_mask(msk, h[2], bit)
            dst = acc if n == 0 else tmp
            o.step(v.tensor_scalar(dst, msk, low, None, ALU.bitwise_and))
            if n:
                o.step(v.tensor_tensor(acc, acc, tmp, ALU.bitwise_xor))
        for j in range(3):
            o.did(v.tensor_tensor(h[j], h[j], acc, ALU.bitwise_xor))
        o.sync()
        for j in range(3):
            o.did(v.tensor_copy(XS[:, j, 0, :], XQ[:, j, :]))
            o.did(v.tensor_copy(XS[:, j, 1:3, :], HX[:, j, :, :]))
        o.sync()
        interleave(XS[:, :, :, :])
        for m, (w, order) in enumerate(((0, (0, 1, 2)), (0, (1, 0, 2)), (1, (0, 1, 2)), (2, (0, 1, 2)))):
            a, b_, c_ = [XS[:, j, w, :] for j in order]
            o.did(v.tensor_scalar(KEY[:, m, :], a, 2, None, ALU.logical_shift_left))
            o.did(v.tensor_scalar(KEYT[:, m, :], b_, 1, None, ALU.logical_shift_left))
            o.sync()
            o.step(v.tensor_tensor(KEY[:, m, :], KEY[:, m, :], KEYT[:, m, :], ALU.bitwise_or))
            o.step(v.tensor_tensor(KEY[:, m, :], KEY[:, m, :], c_, ALU.bitwise_or))
        o.step(v.tensor_scalar(KEYT[:, :, :], KEY[:, :, :], 1 << 29, None, ALU.bitwise_and))
        o.step(v.tensor_scalar(KEYT[:, :, :], KEYT[:, :, :], 1, None, ALU.logical_shift_left))
        o.step(v.tensor_scalar(KEY[:, :, :], KEY[:, :, :], 1 << 29, None, ALU.bitwise_xor))
        v.tensor_tensor(KEY[:, :, :], KEY[:, :, :], KEYT[:, :, :], ALU.bitwise_or).then_inc(key_ready, 1)

        for L in range(2):
            oc = OUTC[L]
            v.wait_ge(weff_mm, 3 * L + 1)
            v.wait_ge(weff_ev, 2 * L + 1)
            v.tensor_tensor(W4[L][:, :], ps_ga[:, 64:64 + oc], WD[L][:, :], ALU.subtract).then_inc(w4_ready, 1)

        for L in range(2):
            oc = OUTC[L]
            v.wait_ge(weff_ev, 2 * L + 2)
            for h in range(HG):
                o.did(v.tensor_scalar(WB[L][:, h, :], WD[L][:, :], headmask[:, h:h + 1], None, ALU.mult))
            o.sync()
            for whole, parts in ((WB[L][:, :, :].rearrange("p h o -> p (h o)"), WBs[L]), (Wcc[L][:, :], Ws[L])):
                for j in range(3):
                    o.step(v.tensor_copy(parts[:, j, :], whole))
                    if j < 2:
                        o.step(v.tensor_tensor(whole, whole, parts[:, j, :], ALU.subtract))
        v.tensor_copy(be[0][0:1, :], be[0][0:1, :]).then_inc(w_split, 1)

        v.wait_ge(x_in, 16)
        for q in range(PAIRS):
            o.did(v.bn_stats(stx[:, q, :], FF[:, PAIRS + q, :]))
        o.sync()
        for q in range(PAIRS):
            ins = v.bn_aggr(mv[0:64, q, :], stx[:, q, :])
        ins.then_inc(ln_var, 1)
        v.wait_ge(ln_std, 1)
        o.step(v.reciprocal(rs[0:64, :, 1], rs[0:64, :, 0]))
        for q in range(PAIRS):
            o.did(v.tensor_scalar(FF[:, q, :], FF[:, PAIRS + q, :], mv[0:64, q, 0:1], rs[0:64, q, 1:2],
                                  ALU.subtract, ALU.mult))
        o.sync()

        v.wait_ge(kcol_ready, 1)
        v.wait_ge(zeros_done, 1)
        plan = [(m, c, kind) for m in range(M) for c in range(CH) for kind in range(3) if kind or c]

        def rank_start(b, w, pair):
            v.wait_ge(kb_in[w], pair * 16 + 16)
            v.tensor_copy(kc_b[:, :, :], kcol[:, :, :, bass.ds(b, 1)].rearrange("p c m b -> p m (c b)"))\
             .then_inc(kc_ready, 1)
            v.wait_ge(kc_ready, b + 1)

        def rank_some(b, w, first, last):
            for n in range(first, last):
                m, c, kind = plan[n]
                key = kc_b[:, m, c:c + 1]
                j = m * CH + c
                row = kb_ring[:, w, m, :]
                if n >= 3:
                    v.wait_ge(compared, b * COMPARES + (n - 2))
                if kind == 0:
                    ins = v.tensor_scalar(cmp[:, n % 3, 0:128 * c], row[:, 0:128 * c], key, None,
                                          ALU.is_le, ALU.add, accum_out=cnt[:, 0, j:j + 1])
                elif kind == 1:
                    ins = v.tensor_scalar(cmp[:, n % 3, 128 * c:N], row[:, 128 * c:N], key, None,
                                          ALU.is_lt, ALU.add, accum_out=cnt[:, 1, j:j + 1])
                else:
                    ins = v.scalar_tensor_tensor(out=cmp[:, n % 3, 0:128],
                                                 in0=row[:, 128 * c:128 * c + 128], scalar=key,
                                                 in1=tri[:, :], op0=ALU.is_equal, op1=ALU.mult,
                                                 accum_out=cnt[:, 2, j:j + 1])
                ins.then_inc(compared, 1)

        def rank_end(b):
            v.wait_ge(compared, b * COMPARES + COMPARES)
            v.tensor_tensor(cnt[:, 1, :], cnt[:, 1, :], cnt[:, 2, :], ALU.add).then_inc(kb_used, 1)
            v.wait_ge(kb_used, 1 + b + 1)
            v.tensor_tensor(rank[:, bass.ds(b, 1), :].rearrange("p a k -> p (a k)"), cnt[:, 0, :], cnt[:, 1, :],
                            ALU.add).then_inc(rank_ready, 1)
            v.wait_ge(rank_ready, b * 2 + 1)
            v.tensor_copy(rank[:, bass.ds(b + B, 1), :], rank[:, bass.ds(b, 1), :]).then_inc(rank_ready, 1)
            v.wait_ge(rank_ready, b * 2 + 2)

        for b in range(4):
            rank_start(b, b % 2, b // 2)
            rank_some(b, b % 2, 0, COMPARES)
            rank_end(b)

        def rank_ahead(n, t, place):
            if t >= 10:
                return
            w, part = t // 5, (t % 5) * 3 + place
            b = (n + 2) * 2 + w
            if part == 0:
                rank_start(b, w, n + 2)
            rank_some(b, w, part * COMPARES // 15, (part + 1) * COMPARES // 15)
            if part == 14:
                rank_end(b)

        def features(n, u):
            src = FF[:, bass.ds(n, 1), :].rearrange("p a n -> p (a n)")
            v.tensor_copy(C2H[0:64, u, 0:N], src).then_inc(prep, 1)
            v.wait_ge(prep, n * 2 + 2)
            v.tensor_tensor(C2H[64:128, u, 0:N], src, C2H[0:64, u, 0:N], ALU.subtract).then_inc(fs_ready, 1)

        def ranks_of(n):
            v.tensor_copy(rank_p[:, :, :], rank[:, bass.ds(n * 2, 2), :]).then_inc(prep, 1)

        def onehots(n, k):
            if k == 0:
                v.wait_ge(prep, n * 2 + 1)
            if k >= 2:
                v.wait_ge(perm_mm, n * 4 + (k - 1))
            for m in range(2):
                for c in range(CH):
                    j = (2 * (k % 2) + m) * CH + c
                    ins = v.tensor_scalar(P1H[:, k % 2, m, c, :], iota[:, :], rank_p[:, k // 2, j:j + 1], None,
                                          ALU.is_equal)
            ins.then_inc(onehot_ready, 1)

        def pads(n, u, b):
            v.wait_ge(perm_ev, n * 4 + (2 * b + 2))
            for p0, p1, from_ in ((0, PADL, PADL), (PADL + N, POSW, PADL + N - 1)):
                ins = v.tensor_copy(R[:, u, b, :, 0, p0:p1],
                                    view(R, slice(0, 128), (u * 2 + b) * 4 * POSW + from_,
                                         [[2 * POSW, 2], [0, p1 - p0]]))
            ins.then_inc(pad_ready, 1)

        def logits(base0, t, g):
            half = (g % 2) * 256
            v.wait_ge(ga_ready, base0 + (g + 1))
            kind = 0 if t == 0 else 1
            ctr = view(ps_ga, slice(0, 128), half + WIN, [[32, BLKS], [1, TOK]])
            v.tensor_tensor(aM[:, :].rearrange("p (k n) -> p k n", k=BLKS), ctr,
                            keymask[:, kind * STEPT:kind * STEPT + STEPT].rearrange("p (k n) -> p k n", k=BLKS),
                            ALU.add).then_inc(am_ready, 1)
            v.wait_ge(am_ready, base0 + (g + 1))
            if g >= 2:
                v.wait_ge(e_ready, base0 + (g - 1))
            so = (g % 2) * NCOL

            def part(k0, nk, n0, nn, i0, ni, q0, qn, qi):
                return v.tensor_tensor(
                    view(S, slice(0, 128), so + (k0 * TOK + n0) * K + i0, [[TOK * K, nk], [K, nn], [1, ni]]),
                    view(ps_ga, slice(0, 128), half + 32 * k0 + q0, [[32, nk], [qn, nn], [qi, ni]]),
                    view(aM, slice(0, 128), k0 * TOK + n0, [[TOK, nk], [1, nn], [0, ni]]), ALU.subtract)

            if t == 0:
                for n in range(5):
                    part(0, 1, n, 1, 0, n + 6 if n < 4 else K, PADL, 1, 1)
                    if n < 4:
                        part(0, 1, n, 1, n + 6, 4 - n, PADL + n + 5, 1, 0)
                part(0, 1, 5, 1, 0, K, 5, 1, 1)
                ins = part(1, BLKS - 1, 0, TOK, 0, K, 0, 1, 1)
            else:
                ins = part(0, BLKS, 0, TOK, 0, K, 0, 1, 1)
            ins.then_inc(s_ready, 1)

        ranks_of(0)
        for k in range(2):
            onehots(0, k)
        features(0, 0)
        for k in range(2, 4):
            onehots(0, k)
        for b in range(2):
            pads(0, 0, b)
        for L in range(2):
            oc = OUTC[L]
            rows = 2 * oc
            with v.Fori(0, PAIRS // 2) as i:
                pairs = steps_of(L, i)
                base0 = pairs[0][2]

                def done(ins, n, k):
                    first = n * FEAT[0] if L == 0 else (n - PAIRS) * FEAT[1] + PAIRS * FEAT[0]
                    ins.then_inc(feat, 1)
                    v.wait_ge(feat, first + k)

                def variance(u, n, base):
                    v.wait_ge(o_used, base + STEPS)
                    v.nop(nofuse=True)
                    v.bn_aggr(mt_[u][0:rows, 0:2], st[u][0:rows, :, :].rearrange("p s k -> p (s k)"))\
                     .then_inc(var_ready, 1)

                def normalise(u, n):
                    v.wait_ge(std_ready, n + 1)
                    v.tensor_tensor(mt_[u][0:rows, 2:3], mt_[u][0:rows, 0:1], be[L][0:rows, :], ALU.add)
                    done(v.reciprocal(mt_[u][0:rows, 1:2], mt_[u][0:rows, 3:4]), n, 1)
                    done(v.tensor_scalar(raw[u][0:rows, 0:N], raw[u][0:rows, 0:N], be[L][0:rows, :],
                                         mt_[u][0:rows, 2:3], ALU.add, ALU.subtract), n, 2)
                    done(v.tensor_scalar(fy[0:rows, :], raw[u][0:rows, 0:N], mt_[u][0:rows, 1:2], None, ALU.mult),
                         n, 3)
                    if L == 0:
                        v.scalar_tensor_tensor(out=FF[:, bass.ds(n + PAIRS, 1), :].rearrange("p a n -> p (a n)"),
                                               in0=fy[0:rows, :], scalar=0.2, in1=fy[0:rows, :],
                                               op0=ALU.mult, op1=ALU.max).then_inc(pair_done, 1)
                    else:
                        v.scalar_tensor_tensor(out=F2[:, :], in0=fy[:, :], scalar=0.2, in1=fy[:, :],
                                               op0=ALU.mult, op1=ALU.max).then_inc(f2_ready, 1)

                def conv_variance(u, n):
                    v.wait_ge(h3_mm, n - (PAIRS - 1))
                    done(v.bn_stats(mh[u][:, 4:10], ps_t32[0:64, :]), n, 4)
                    v.nop(nofuse=True)
                    v.bn_aggr(mh[u][:, 0:2], mh[u][:, 4:10]).then_inc(var3_ready, 1)

                def finish(u, n):
                    v.wait_ge(std3_ready, n - (PAIRS - 1))
                    done(v.reciprocal(mh[u][:, 3:4], mh[u][:, 2:3]), n, 5)
                    done(v.tensor_scalar(F2[0:64, :], ps_t32[0:64, :], mh[u][:, 0:1], mh[u][:, 3:4],
                                         ALU.subtract, ALU.mult), n, 6)
                    done(v.scalar_tensor_tensor(out=fy[0:64, :], in0=F2[0:64, :], scalar=0.2, in1=F2[0:64, :],
                                                op0=ALU.mult, op1=ALU.max), n, 7)
                    v.wait_ge(xt_in, (n - PAIRS) * 48 + 48)
                    v.tensor_tensor(FF[:, bass.ds(n, 1), :].rearrange("p a n -> p (a n)"), xt[:, :], fy[0:64, :],
                                    ALU.add).then_inc(pair_done, 1)

                for T in range(TICKS):
                    if place(T, 0):
                        u, t, g = place(T, 0)
                        logits(base0, t, g)
                        if L == 0:
                            rank_ahead(pairs[u][1], t, 0)
                    if place(T, 1):
                        u, t, g = place(T, 1)
                        v.wait_ge(mb_ready, base0 + (g + 1))
                        v.tensor_tensor(S[:, g % 2, :], S[:, g % 2, :], ps_mb[:, 0:NCOL], ALU.subtract)\
                         .then_inc(d_ready, 1)
                    if place(T, 0):
                        u, t, g = place(T, 0)
                        v.wait_ge(mt_ready, base0 + (g + 1))
                        if g >= 1:
                            v.wait_ge(mte_ready, base0 + g)
                        v.tensor_reduce(view(MTs, slice(0, 120), 0, [[HG, 8], [1, HG]]),
                                        view(ps_mt, slice(0, 120), 0, [[HG * WIN, 8], [1, HG], [HG, WIN]]),
                                        AX, ALU.max).then_inc(mts_ready, 1)
                    if L == 0 and place(T, 0):
                        rank_ahead(pairs[place(T, 0)[0]][1], place(T, 0)[1], 1)
                    if place(T, 4):
                        u, t, g = place(T, 4)
                        v.wait_ge(o_ready, base0 + (g + 1))
                        v.tensor_reduce(raw[u][0:rows, t * STEPT:t * STEPT + STEPT],
                                        ps_o[g % 2][0:rows, 0:NCOL].rearrange("p (n i) -> p n i", i=K), AX, ALU.max)
                        real = STEPT if t < STEPS - 1 else LASTT
                        v.bn_stats(st[u][0:rows, t, :], ps_o[g % 2][0:rows, 0:real * K]).then_inc(o_used, 1)
                    if place(T, 0):
                        u, t, g = place(T, 0)
                        n1 = pairs[u][1] + 1
                        if L == 0:
                            rank_ahead(pairs[u][1], t, 2)
                        if t == 0:
                            ranks_of(n1)
                        if t in (1, 3, 5, 6):
                            onehots(n1, (1, 3, 5, 6).index(t))
                        if t == 3:
                            if u == 1:
                                v.wait_ge(o_ready, pairs[u][2])
                            features(n1, 1 - u)
                        if t in (6, 8):
                            pads(n1, 1 - u, (t - 6) // 2)
                    if T == STEPS + 3:
                        variance(0, pairs[0][1], pairs[0][2])
                    if T == STEPS + 4:
                        normalise(0, pairs[0][1])
                    if L == 1 and T == STEPS + 9:
                        conv_variance(0, pairs[0][1])
                    if L == 1 and T == STEPS + 10:
                        finish(0, pairs[0][1])
                variance(1, pairs[1][1], pairs[1][2])
                normalise(1, pairs[1][1])
                if L == 1:
                    conv_variance(1, pairs[1][1])
                    finish(1, pairs[1][1])
        v.wait_ge(pair_done, 1 + 2 * PAIRS)
        v.memset(C2H[0:1, 0, 0:1], 0.0).then_inc(graph_done, 1)

        def layernorm(n):
            for t in range(TILES):
                o.did(v.bn_stats(st2[:, t, :], XN[:, t, :]))
            o.sync()
            for t in range(TILES):
                ins = v.bn_aggr(mv2[:, t, :], st2[:, t, :])
            ins.then_inc(ln2_var, 1)
            v.wait_ge(ln2_std, n)
            o.step(v.reciprocal(rs2[:, :, 1], rs2[:, :, 0]))
            for t in range(TILES):
                ins = v.tensor_scalar(LN[:, t, :], XN[:, t, :], mv2[:, t, 0:1], rs2[:, t, 1:2],
                                      ALU.subtract, ALU.mult)
            ins.then_inc(ln2_ready, 1)

        v.wait_ge(graph_done, 1)
        v.wait_ge(xn_in, 32)
        layernorm(1)
        v.wait_ge(aw_in, 16 * 7)
        pos = lambda r: view(cosT, r, 0, [[0, B], [1, C]])
        snv = lambda r: view(sinT, r, 0, [[0, B], [1, C]])
        by_b = lambda a: a.rearrange("p (b s) -> p b s", b=B)
        with v.Fori(0, NGRP) as g:
            for j in range(REP + 1):
                if j == 0:
                    v.tensor_copy(bg[:, 0:1], bk[:, bass.ds(g, 1)]).then_inc(bg_ready, 1)
                    v.tensor_copy(bg[:, 1:REP + 1], bq[:, bass.ds(g * REP, REP)]).then_inc(bg_ready, 1)
                    v.wait_ge(bg_ready, g * 2 + 2)
                bank = ps[4 + j % 2]
                v.wait_ge(proj_mm, g * (REP + 1) + (j + 1))
                if j >= 2:
                    v.wait_ge(qk_ready, 1 + g * (REP + 1) + (j - 1))
                else:
                    v.wait_ge(qk_ready, 1 + g * (REP + 1))
                v.scalar_tensor_tensor(out=by_b(r1[:, j % 2, :]), in0=by_b(bank[:, :]), scalar=bg[:, j:j + 1],
                                       in1=pos(slice(0, 128)), op0=ALU.add, op1=ALU.mult)
                v.scalar_tensor_tensor(out=by_b(r2[0:64, j % 2, :]), in0=by_b(bank[64:128, :]),
                                       scalar=bg[64:128, j:j + 1], in1=snv(slice(64, 128)),
                                       op0=ALU.add, op1=ALU.mult)
                v.scalar_tensor_tensor(out=by_b(r2[64:128, j % 2, :]), in0=by_b(bank[0:64, :]),
                                       scalar=bg[0:64, j:j + 1], in1=snv(slice(0, 64)),
                                       op0=ALU.add, op1=ALU.mult).then_inc(rope_parts, 1)
            v.wait_ge(sc_mm, 1 + g + 1)
            v.scalar_tensor_tensor(out=pr[:, :, :], in0=by_b(ps_sc[:, :]), scalar=1.0 / math.sqrt(DH),
                                   in1=view(causal, slice(0, 128), 0, [[0, B], [1, C]]), op0=ALU.mult, op1=ALU.add)\
             .then_inc(soft, 1)
            v.wait_ge(soft, g * SOFT + 1)
            v.tensor_reduce(pm[:, 0, :], pr[:, :, :], AX, ALU.max).then_inc(soft, 1)
            v.wait_ge(soft, g * SOFT + 2)
            v.tensor_tensor(pr[:, :, :], pr[:, :, :], view(pm, slice(0, 128), 0, [[1, B], [0, C]]), ALU.subtract)\
             .then_inc(sm_ready, 1)
            v.wait_ge(ex_ready, g + 1)
            v.tensor_reduce(pm[:, 1, :], pr[:, :, :], AX, ALU.add).then_inc(soft, 1)
            v.wait_ge(soft, g * SOFT + 3)
            v.reciprocal(pm[:, 2, :], pm[:, 1, :]).then_inc(soft, 1)
            v.wait_ge(soft, g * SOFT + 4)
            v.tensor_tensor(pr[:, :, :], pr[:, :, :], view(pm, slice(0, 128), 2 * B, [[1, B], [0, C]]), ALU.mult)\
             .then_inc(pr_ready, 1)
        v.wait_ge(wo_used, 1 + NGRP)
        for t in range(TILES):
            o.did(v.tensor_tensor(XN[:, t, :], ps[t][:, :], XN[:, t, :], ALU.add))
        o.sync()
        layernorm(2)

        def did(ins):
            ins.then_inc(ffn_vec, 1)

        v.wait_ge(ln2_ready, 2)
        for t in range(TILES):
            o.did(v.bn_stats(st2[:, t, :], LN[:, t, :]))
        o.sync()
        v.wait_ge(ffn_act, 4)
        o.step(v.tensor_tensor(gl[:, 1, :], gl[:, 0, :], gl[:, 0, :], ALU.mult))
        o.step(v.tensor_scalar(gl[:, 1, :], gl[:, 1, :], 0.044715, 1.0, ALU.mult, ALU.add))
        did(v.tensor_tensor(gl[:, 1, :], gl[:, 1, :], gl[:, 0, :], ALU.mult))
        for t in range(TILES):
            ins = v.bn_aggr(mv2[:, t, :], st2[:, t, :])
        did(ins)
        v.wait_ge(ffn_act, 7)
        o.step(v.tensor_scalar(gl[:, 2, :], gl[:, 2, :], 1.0, 0.5, ALU.add, ALU.mult))
        did(v.tensor_tensor(gl[:, 3, :], gl[:, 2, :], gl[:, 0, :], ALU.mult))
        v.wait_ge(ffn_mm, 8)
        v.wait_ge(fw_in, 16 * 13)
        lr = view(lrel, slice(0, 128), 0, [[0, TILES], [1, NSLOT]])
        by_t = lambda a: a.rearrange("p (t k) -> p t k", t=TILES)
        o.did(v.scalar_tensor_tensor(out=rt[:, :, :], in0=by_t(ps[3][:, :]), scalar=1.0 / math.sqrt(RDIM), in1=lr,
                                     op0=ALU.mult, op1=ALU.add))
        o.did(v.scalar_tensor_tensor(out=at[:, :, :], in0=by_t(ps[4][:, :]), scalar=1.0 / math.sqrt(BOT), in1=lr,
                                     op0=ALU.mult, op1=ALU.add))
        o.sync()
        for t in range(TILES):
            o.did(v.max(top[:, t, :], rt[:, t, :]))
        o.sync()
        for t in range(TILES):
            o.did(v.match_replace(rp[:, t, :], top[:, t, :], rt[:, t, :], -3e38))
        o.sync()
        o.step(v.tensor_tensor(rp[:, :, :], rp[:, :, :], rt[:, :, :], ALU.is_equal))
        o.step(v.scalar_tensor_tensor(out=at[:, :, :], in0=rp[:, :, :], scalar=-1e30, in1=at[:, :, :],
                                      op0=ALU.mult, op1=ALU.add))
        o.step(v.tensor_reduce(gt[:, 1, :], at[:, :, :], AX, ALU.max))
        did(v.tensor_tensor(at[:, :, :], at[:, :, :], view(gt, slice(0, 128), 1 * TILES, [[1, TILES], [0, NSLOT]]),
                            ALU.subtract))
        v.wait_ge(ffn_mm, 9)
        did(v.tensor_scalar(gt[:, 3, :], ps[6][:, 8:8 + TILES], sc3[:, 0:1], None, ALU.add))
        o.step(v.tensor_reduce(gt[:, 2, 0:1], ps[6][:, 0:TILES], AX, ALU.add))
        o.step(v.tensor_scalar(gt[:, 2, 1:2], gt[:, 2, 0:1], 1.0 / TOKENS, 1e-6, ALU.mult, ALU.add))
        o.step(v.reciprocal(gt[:, 2, 2:3], gt[:, 2, 1:2]))
        o.step(v.tensor_scalar(gt[:, 5, :], gt[:, 0, :], gt[:, 2, 2:3], 0.5, ALU.mult, ALU.mult))
        v.wait_ge(ffn_act, 10)
        o.step(v.scalar_tensor_tensor(out=gt[:, 5, :], in0=gt[:, 4, :], scalar=2.5, in1=gt[:, 5, :],
                                      op0=ALU.mult, op1=ALU.add))
        o.step(v.tensor_scalar(gt[:, 5, :], gt[:, 5, :], 0.0, 5.0, ALU.max, ALU.min))
        o.step(v.tensor_scalar(gt[:, 5, :], gt[:, 5, :], 0.5, 1.0 / 1.5, ALU.subtract, ALU.mult))
        o.step(v.tensor_scalar(gt[:, 5, :], gt[:, 5, :], 0.0, 1.0, ALU.max, ALU.min))
        did(v.tensor_scalar(gt[:, 6, :], gt[:, 5, :], 0.0, None, ALU.add))
        v.wait_ge(ffn_vec, 6)
        did(v.tensor_scalar(gt[:, 7, :], gt[:, 5, :], sc3[:, 1:2], sc3[:, 2:3], ALU.mult, ALU.add))
        v.wait_ge(ffn_act, 9)
        o.step(v.tensor_reduce(gt[:, 9, :], at[:, :, :], AX, ALU.add))
        o.step(v.reciprocal(gt[:, 10, :], gt[:, 9, :]))
        did(v.tensor_tensor(at[:, :, :], at[:, :, :], view(gt, slice(0, 128), 10 * TILES, [[1, TILES], [0, NSLOT]]),
                            ALU.mult))
        v.wait_ge(ffn_act, 11)
        o.step(v.tensor_scalar(gt[:, 6, :], gt[:, 8, :], 0.05, None, ALU.is_ge))
        o.step(v.tensor_tensor(gt[:, 11, :], gt[:, 8, :], gt[:, 6, :], ALU.mult))
        for t in range(TILES):
            o.did(v.tensor_tensor(XN[:, t, :], XN[:, t, :], LN[:, t, :], ALU.add))
        o.sync()
        for t in range(TILES):
            v.wait_ge(ffn_mm, 11 + t)
            ins = v.scalar_tensor_tensor(out=XN[:, t, :], in0=ps[t][:, :], scalar=gt[:, 11, t:t + 1],
                                         in1=XN[:, t, :], op0=ALU.mult, op1=ALU.add)
            ins.then_inc(row_ready, 1)

    ctx.close()


def kernel(**inputs):
    import numpy as _np
    import concourse.bacc as _bacc
    from concourse import mybir as _mybir
    from concourse.bass_utils import run_bass_kernel_spmd as _run

    a = {n: _np.asarray(x) for n, x in inputs.items()}
    pre, att, ffn = "L0_xattn_", "L0_attn_", "L0_ffn_"
    data = {
        "x": a["x"], "ctx_4096": a["ctx_4096"],
        "wlin0": a[pre + "W_lin1"], "wlin1": a[pre + "W_lin2"],
        "wconv0T": a[pre + "W_conv1"].T, "wconv1T": a[pre + "W_conv2"].T, "wconv3T": a[pre + "W_conv3"].T,
        "blin0": a[pre + "b_lin1"], "blin1": a[pre + "b_lin2"],
        "Wq": a[att + "Wq"], "Wk": a[att + "Wk"], "Wv": a[att + "Wv"], "Wo": a[att + "Wo"],
        "bqT": a[att + "bq"].reshape(NHEAD, DH).T, "bkT": a[att + "bk"].reshape(NGRP, DH).T,
        "bv": a[att + "bv"], "bo": a[att + "bo"],
        "fWqT": a[ffn + "Wq"].T, "WrT": a[ffn + "Wr"].T, "akT": a[ffn + "aux_keys"].T,
        "avT": a[ffn + "aux_values"].T, "WvdT": a[ffn + "Wvd"].T, "WvuT": a[ffn + "Wvu"].T,
        "Wu1T": a[ffn + "Wu1"].T, "bu1": a[ffn + "bu1"], "Wu2T": a[ffn + "Wu2"].T, "bu2": a[ffn + "bu2"],
        "gate_w1": a[ffn + "gate_w1"].reshape(1), "gate_bias": a[ffn + "gate_bias"].reshape(1),
        "log_rel": a[ffn + "log_rel"],
    }
    data.update(constants())
    nc = _bacc.Bacc("TRN2", target_bir_lowering=False, num_devices=1)
    arrays, io = {}, {}
    for name, v in data.items():
        v = _np.ascontiguousarray(v)
        arrays[f"in_{name}"] = v
        io[name] = nc.dram_tensor(f"in_{name}", v.shape, _mybir.dt.from_np(v.dtype), kind="ExternalInput").ap()
    out = nc.dram_tensor("out_0", (B, C, N), _mybir.dt.float32, kind="ExternalOutput").ap()
    build(nc, io, out)
    r = _run(nc, [arrays], core_ids=[0])
    return r.results[0]["out_0"]
```
